# Optimizing a Trainium2 kernel written in Bass

```python
import numpy as np
import jax
import jax.numpy as jnp

def _softmax(x, axis=-1):
    return jax.nn.softmax(x, axis=axis)

def _gelu(x):
    return jax.nn.gelu(x, approximate=True)

def _silu(x):
    return jax.nn.silu(x)

def _sigmoid(x):
    return jax.nn.sigmoid(x)

def _layernorm(x, axis=-1, eps=1e-05):
    m = jnp.mean(x, axis=axis, keepdims=True)
    v = jnp.var(x, axis=axis, keepdims=True)
    return (x - m) / jnp.sqrt(v + eps)

def _scatter_add(tgt, idx, src, axis=0):
    return tgt.at[idx].add(src)

def _segment_sum(src, seg, n):
    return jax.ops.segment_sum(src, seg, n)
kernel_name = 'mk_decoder_preln_d1_seqx_r4_569246'

def setup_inputs(seed: int=0):
    np.random.seed(seed)
    _w = jnp.asarray

    def _rec_inputs():
        import jax
        import jax.numpy as jnp
        _rk = jax.random.key(seed)
        x = -0.0002928 + 1 * jax.random.normal(jax.random.fold_in(_rk, 1), (4, 1024, 256), jnp.float32)
        _lenS = 1024 - jax.random.randint(jax.random.fold_in(_rk, 7), (4,), 0, max(1, 1024 // 4) + 1, jnp.int32)
        _lenS2 = 154 - jax.random.randint(jax.random.fold_in(_rk, 8), (4,), 0, max(1, 154 // 4) + 1, jnp.int32)
        _ctx_1024P = jax.random.normal(jax.random.fold_in(_rk, 11), (4, 16, 256), jnp.float32)
        _ctx_1024c = jax.random.dirichlet(jax.random.fold_in(_rk, 511), 0.3 * jnp.ones((16,), jnp.float32), (4, 154))
        _ctx_1024t = jnp.einsum('bsk,bkd->bsd', _ctx_1024c, _ctx_1024P)
        _ctx_1024t = _ctx_1024t * jax.lax.rsqrt(jnp.mean(jnp.square(_ctx_1024t)) + 1e-12) * 0.953939
        ctx_1024 = -1.39393e-06 + 0.999914 * (_ctx_1024t + 0.3 * jax.random.normal(jax.random.fold_in(_rk, 611), (4, 154, 256), jnp.float32))
        return (x, ctx_1024)
    x, ctx_1024 = _rec_inputs()

    def _L0_attn_setup():
        import jax, jax.numpy as jnp
        import numpy as np
        B, T, H = (2, 512, 256)
        EXPAND, N = (2, 16)
        DIN = H * EXPAND
        EPS = 1e-06

        def rmsnorm(x, w):
            var = jnp.mean(x * x, axis=-1, keepdims=True)
            return x * jax.lax.rsqrt(var + EPS) * w

        def liquid_scan(x_in, a_mod, a_base, B_in, C_in):

            def step(h, inp):
                a_t, b_t, c_t, x_t = inp
                h = a_t[:, :, None] * a_base * h + b_t[:, None, :] * x_t[:, :, None]
                y_t = jnp.einsum('bdn,bn->bd', h, c_t)
                return (h, y_t)
            h0 = jnp.zeros((x_in.shape[0], DIN, N), x_in.dtype)
            xs = (jnp.swapaxes(a_mod, 0, 1), jnp.swapaxes(B_in, 0, 1), jnp.swapaxes(C_in, 0, 1), jnp.swapaxes(x_in, 0, 1))
            _, ys = jax.lax.scan(step, h0, xs)
            return jnp.swapaxes(ys, 0, 1)
        key = jax.random.key(seed)
        ks = jax.random.split(key, 9)
        s_h = 1.0 / np.sqrt(H)
        s_d = 1.0 / np.sqrt(DIN)
        return {'x': jax.random.normal(ks[0], (B, T, H), jnp.float32), 'norm_w': jnp.ones((H,), jnp.float32), 'in_proj_w': jax.random.normal(ks[1], (H, 2 * DIN), jnp.float32) * s_h, 'A_proj_w': jax.random.normal(ks[2], (DIN, DIN), jnp.float32) * s_d, 'A_proj_b': jax.random.normal(ks[3], (DIN,), jnp.float32) * 0.02, 'A_base': jnp.log(jnp.arange(1, N + 1, dtype=jnp.float32)), 'B_proj_w': jax.random.normal(ks[4], (DIN, N), jnp.float32) * s_d, 'C_proj_w': jax.random.normal(ks[5], (DIN, N), jnp.float32) * s_d, 'D': jnp.ones((DIN,), jnp.float32), 'out_proj_w': jax.random.normal(ks[6], (DIN, H), jnp.float32) * s_d}
    _L0_attn_all = _L0_attn_setup()
    _L0_attn_in = {k: v for k, v in _L0_attn_all.items() if k in ('norm_w', 'in_proj_w', 'A_proj_w', 'A_proj_b', 'A_base', 'B_proj_w', 'C_proj_w', 'D', 'out_proj_w')}
    del _L0_attn_all

    def _L0_xattn_setup():
        import jax, jax.numpy as jnp
        import numpy as np
        D_MODEL = 256
        NUM_HEADS = 16
        DEPTH = D_MODEL // NUM_HEADS

        def _split_heads(x):
            B, S, _ = x.shape
            return x.reshape(B, S, NUM_HEADS, DEPTH).transpose(0, 2, 1, 3)
        key = jax.random.key(seed)
        ks = jax.random.split(key, 8)
        B, S, D = (2, 512, D_MODEL)
        s = 1.0 / np.sqrt(D)
        return {'q': jax.random.normal(ks[0], (B, S, D), jnp.float32), 'k': jax.random.normal(ks[1], (B, S, D), jnp.float32), 'v': jax.random.normal(ks[2], (B, S, D), jnp.float32), 'Wq': jax.random.normal(ks[3], (D, D), jnp.float32) * s, 'bq': jnp.zeros((D,), jnp.float32), 'Wk': jax.random.normal(ks[4], (D, D), jnp.float32) * s, 'bk': jnp.zeros((D,), jnp.float32), 'Wv': jax.random.normal(ks[5], (D, D), jnp.float32) * s, 'bv': jnp.zeros((D,), jnp.float32), 'Wo': jax.random.normal(ks[6], (D, D), jnp.float32) * s, 'bo': jnp.zeros((D,), jnp.float32)}
    _L0_xattn_all = _L0_xattn_setup()
    _L0_xattn_in = {k: v for k, v in _L0_xattn_all.items() if k in ('Wq', 'bq', 'Wk', 'bk', 'Wv', 'bv', 'Wo', 'bo')}
    del _L0_xattn_all

    def _L0_ffn_setup():
        import jax, jax.numpy as jnp
        import numpy as np
        EPS = 1e-05
        N_HEADS = 16
        TOP_K = 2

        def _ln(x, g, b):
            m = x.mean(-1, keepdims=True)
            v = ((x - m) ** 2).mean(-1, keepdims=True)
            return (x - m) / jnp.sqrt(v + EPS) * g + b

        def _block_fwd(x, ln1_g, ln1_b, ln2_g, ln2_b, Wq, bq, Wk, bk, Wv, bv, Wo, bo, Wr, br, e_w1, e_b1, e_w2, e_b2):
            B, S, D = x.shape
            H = N_HEADS
            hd = D // H
            h = _ln(x, ln1_g, ln1_b)
            q = (h @ Wq + bq).reshape(B, S, H, hd).transpose(0, 2, 1, 3)
            k = (h @ Wk + bk).reshape(B, S, H, hd).transpose(0, 2, 1, 3)
            v = (h @ Wv + bv).reshape(B, S, H, hd).transpose(0, 2, 1, 3)
            scores = jnp.einsum('bhqd,bhkd->bhqk', q, k) / hd ** 0.5
            causal = jnp.tril(jnp.ones((S, S), dtype=bool))
            scores = jnp.where(causal, scores, -jnp.inf)
            attn = jax.nn.softmax(scores, axis=-1)
            o = jnp.einsum('bhqk,bhkd->bhqd', attn, v).transpose(0, 2, 1, 3).reshape(B, S, D)
            a = o @ Wo + bo + x
            h2 = _ln(a, ln2_g, ln2_b)
            logits = h2 @ Wr + br
            topv = jax.lax.top_k(logits, TOP_K)[0]
            kmask = logits >= topv[..., -1:]
            w = jax.nn.softmax(jnp.where(kmask, logits, -jnp.inf), axis=-1)
            mid = jax.nn.gelu(jnp.einsum('bsd,edf->bsef', h2, e_w1) + e_b1, approximate=False)
            eo = jnp.einsum('bsef,efd->bsed', mid, e_w2) + e_b2
            moe = jnp.einsum('bse,bsed->bsd', w, eo)
            return moe + a
        key = jax.random.key(seed)
        B, S, D, E = (1, 512, 256, 8)
        F = 4 * D
        ks = jax.random.split(key, 8)

        def n(k, shape):
            return jax.random.normal(k, shape, jnp.float32) * 0.02
        return dict(x=jax.random.normal(ks[0], (B, S, D), jnp.float32), ln1_g=jnp.ones((D,), jnp.float32), ln1_b=jnp.zeros((D,), jnp.float32), ln2_g=jnp.ones((D,), jnp.float32), ln2_b=jnp.zeros((D,), jnp.float32), Wq=n(ks[1], (D, D)), bq=jnp.zeros((D,), jnp.float32), Wk=n(ks[2], (D, D)), bk=jnp.zeros((D,), jnp.float32), Wv=n(ks[3], (D, D)), bv=jnp.zeros((D,), jnp.float32), Wo=n(ks[4], (D, D)), bo=jnp.zeros((D,), jnp.float32), Wr=n(ks[5], (D, E)), br=jnp.zeros((E,), jnp.float32), e_w1=n(ks[6], (E, D, F)), e_b1=jnp.zeros((E, F), jnp.float32), e_w2=n(ks[7], (E, F, D)), e_b2=jnp.zeros((E, D), jnp.float32))
    _L0_ffn_all = _L0_ffn_setup()
    _L0_ffn_in = {k: v for k, v in _L0_ffn_all.items() if k in ('ln1_g', 'ln1_b', 'ln2_g', 'ln2_b', 'Wq', 'bq', 'Wk', 'bk', 'Wv', 'bv', 'Wo', 'bo', 'Wr', 'br', 'e_w1', 'e_b1', 'e_w2', 'e_b2')}
    del _L0_ffn_all
    return {'x': x, 'ctx_1024': ctx_1024, 'L0_attn_norm_w': _L0_attn_in['norm_w'], 'L0_attn_in_proj_w': _L0_attn_in['in_proj_w'], 'L0_attn_A_proj_w': _L0_attn_in['A_proj_w'], 'L0_attn_A_proj_b': _L0_attn_in['A_proj_b'], 'L0_attn_A_base': _L0_attn_in['A_base'], 'L0_attn_B_proj_w': _L0_attn_in['B_proj_w'], 'L0_attn_C_proj_w': _L0_attn_in['C_proj_w'], 'L0_attn_D': _L0_attn_in['D'], 'L0_attn_out_proj_w': _L0_attn_in['out_proj_w'], 'L0_xattn_Wq': _L0_xattn_in['Wq'], 'L0_xattn_bq': _L0_xattn_in['bq'], 'L0_xattn_Wk': _L0_xattn_in['Wk'], 'L0_xattn_bk': _L0_xattn_in['bk'], 'L0_xattn_Wv': _L0_xattn_in['Wv'], 'L0_xattn_bv': _L0_xattn_in['bv'], 'L0_xattn_Wo': _L0_xattn_in['Wo'], 'L0_xattn_bo': _L0_xattn_in['bo'], 'L0_ffn_ln1_g': _L0_ffn_in['ln1_g'], 'L0_ffn_ln1_b': _L0_ffn_in['ln1_b'], 'L0_ffn_ln2_g': _L0_ffn_in['ln2_g'], 'L0_ffn_ln2_b': _L0_ffn_in['ln2_b'], 'L0_ffn_Wq': _L0_ffn_in['Wq'], 'L0_ffn_bq': _L0_ffn_in['bq'], 'L0_ffn_Wk': _L0_ffn_in['Wk'], 'L0_ffn_bk': _L0_ffn_in['bk'], 'L0_ffn_Wv': _L0_ffn_in['Wv'], 'L0_ffn_bv': _L0_ffn_in['bv'], 'L0_ffn_Wo': _L0_ffn_in['Wo'], 'L0_ffn_bo': _L0_ffn_in['bo'], 'L0_ffn_Wr': _L0_ffn_in['Wr'], 'L0_ffn_br': _L0_ffn_in['br'], 'L0_ffn_e_w1': _L0_ffn_in['e_w1'], 'L0_ffn_e_b1': _L0_ffn_in['e_b1'], 'L0_ffn_e_w2': _L0_ffn_in['e_w2'], 'L0_ffn_e_b2': _L0_ffn_in['e_b2']}

def reference(x, ctx_1024, L0_attn_norm_w, L0_attn_in_proj_w, L0_attn_A_proj_w, L0_attn_A_proj_b, L0_attn_A_base, L0_attn_B_proj_w, L0_attn_C_proj_w, L0_attn_D, L0_attn_out_proj_w, L0_xattn_Wq, L0_xattn_bq, L0_xattn_Wk, L0_xattn_bk, L0_xattn_Wv, L0_xattn_bv, L0_xattn_Wo, L0_xattn_bo, L0_ffn_ln1_g, L0_ffn_ln1_b, L0_ffn_ln2_g, L0_ffn_ln2_b, L0_ffn_Wq, L0_ffn_bq, L0_ffn_Wk, L0_ffn_bk, L0_ffn_Wv, L0_ffn_bv, L0_ffn_Wo, L0_ffn_bo, L0_ffn_Wr, L0_ffn_br, L0_ffn_e_w1, L0_ffn_e_b1, L0_ffn_e_w2, L0_ffn_e_b2):
    import jax
    import jax.numpy as jnp

    def _L0_attn_ref(x, norm_w, in_proj_w, A_proj_w, A_proj_b, A_base, B_proj_w, C_proj_w, D, out_proj_w):
        import jax, jax.numpy as jnp
        import numpy as np
        B, T, H = (2, 512, 256)
        EXPAND, N = (2, 16)
        DIN = H * EXPAND
        EPS = 1e-06

        def rmsnorm(x, w):
            var = jnp.mean(x * x, axis=-1, keepdims=True)
            return x * jax.lax.rsqrt(var + EPS) * w

        def liquid_scan(x_in, a_mod, a_base, B_in, C_in):

            def step(h, inp):
                a_t, b_t, c_t, x_t = inp
                h = a_t[:, :, None] * a_base * h + b_t[:, None, :] * x_t[:, :, None]
                y_t = jnp.einsum('bdn,bn->bd', h, c_t)
                return (h, y_t)
            h0 = jnp.zeros((x_in.shape[0], DIN, N), x_in.dtype)
            xs = (jnp.swapaxes(a_mod, 0, 1), jnp.swapaxes(B_in, 0, 1), jnp.swapaxes(C_in, 0, 1), jnp.swapaxes(x_in, 0, 1))
            _, ys = jax.lax.scan(step, h0, xs)
            return jnp.swapaxes(ys, 0, 1)
        residual = x
        xn = rmsnorm(x, norm_w)
        xz = xn @ in_proj_w
        x_in, z = jnp.split(xz, 2, axis=-1)
        x_in = jax.nn.silu(x_in)
        a_mod = jax.nn.sigmoid(x_in @ A_proj_w + A_proj_b)
        a_base = jax.nn.sigmoid(A_base)
        B_in = x_in @ B_proj_w
        C_in = x_in @ C_proj_w
        y = liquid_scan(x_in, a_mod, a_base, B_in, C_in)
        y = (y + D * x_in) * jax.nn.silu(z)
        return residual + y @ out_proj_w

    def _L0_xattn_ref(q, k, v, Wq, bq, Wk, bk, Wv, bv, Wo, bo):
        import jax, jax.numpy as jnp
        import numpy as np
        D_MODEL = 256
        NUM_HEADS = 16
        DEPTH = D_MODEL // NUM_HEADS

        def _split_heads(x):
            B, S, _ = x.shape
            return x.reshape(B, S, NUM_HEADS, DEPTH).transpose(0, 2, 1, 3)
        qh = _split_heads(q @ Wq + bq)
        kh = _split_heads(k @ Wk + bk)
        vh = _split_heads(v @ Wv + bv)
        scale = 1.0 / jnp.sqrt(jnp.float32(DEPTH))
        logits = jnp.einsum('bhqd,bhkd->bhqk', qh, kh) * scale
        weights = jax.nn.softmax(logits, axis=-1)
        attn = jnp.einsum('bhqk,bhkd->bhqd', weights, vh)
        B, H, S, d = attn.shape
        attn = attn.transpose(0, 2, 1, 3).reshape(B, S, H * d)
        return attn @ Wo + bo

    def _L0_ffn_ref(x, ln1_g, ln1_b, ln2_g, ln2_b, Wq, bq, Wk, bk, Wv, bv, Wo, bo, Wr, br, e_w1, e_b1, e_w2, e_b2):
        import jax, jax.numpy as jnp
        import numpy as np
        EPS = 1e-05
        N_HEADS = 16
        TOP_K = 2

        def _ln(x, g, b):
            m = x.mean(-1, keepdims=True)
            v = ((x - m) ** 2).mean(-1, keepdims=True)
            return (x - m) / jnp.sqrt(v + EPS) * g + b

        def _block_fwd(x, ln1_g, ln1_b, ln2_g, ln2_b, Wq, bq, Wk, bk, Wv, bv, Wo, bo, Wr, br, e_w1, e_b1, e_w2, e_b2):
            B, S, D = x.shape
            H = N_HEADS
            hd = D // H
            h = _ln(x, ln1_g, ln1_b)
            q = (h @ Wq + bq).reshape(B, S, H, hd).transpose(0, 2, 1, 3)
            k = (h @ Wk + bk).reshape(B, S, H, hd).transpose(0, 2, 1, 3)
            v = (h @ Wv + bv).reshape(B, S, H, hd).transpose(0, 2, 1, 3)
            scores = jnp.einsum('bhqd,bhkd->bhqk', q, k) / hd ** 0.5
            causal = jnp.tril(jnp.ones((S, S), dtype=bool))
            scores = jnp.where(causal, scores, -jnp.inf)
            attn = jax.nn.softmax(scores, axis=-1)
            o = jnp.einsum('bhqk,bhkd->bhqd', attn, v).transpose(0, 2, 1, 3).reshape(B, S, D)
            a = o @ Wo + bo + x
            h2 = _ln(a, ln2_g, ln2_b)
            logits = h2 @ Wr + br
            topv = jax.lax.top_k(logits, TOP_K)[0]
            kmask = logits >= topv[..., -1:]
            w = jax.nn.softmax(jnp.where(kmask, logits, -jnp.inf), axis=-1)
            mid = jax.nn.gelu(jnp.einsum('bsd,edf->bsef', h2, e_w1) + e_b1, approximate=False)
            eo = jnp.einsum('bsef,efd->bsed', mid, e_w2) + e_b2
            moe = jnp.einsum('bse,bsed->bsd', w, eo)
            return moe + a
        return _block_fwd(x, ln1_g, ln1_b, ln2_g, ln2_b, Wq, bq, Wk, bk, Wv, bv, Wo, bo, Wr, br, e_w1, e_b1, e_w2, e_b2)
    x = x + _L0_attn_ref(_layernorm(x, axis=-1), L0_attn_norm_w, L0_attn_in_proj_w, L0_attn_A_proj_w, L0_attn_A_proj_b, L0_attn_A_base, L0_attn_B_proj_w, L0_attn_C_proj_w, L0_attn_D, L0_attn_out_proj_w)
    x = x + _L0_xattn_ref(_layernorm(x, axis=-1), ctx_1024, ctx_1024, L0_xattn_Wq, L0_xattn_bq, L0_xattn_Wk, L0_xattn_bk, L0_xattn_Wv, L0_xattn_bv, L0_xattn_Wo, L0_xattn_bo)
    x = x + _L0_ffn_ref(_layernorm(x, axis=-1), L0_ffn_ln1_g, L0_ffn_ln1_b, L0_ffn_ln2_g, L0_ffn_ln2_b, L0_ffn_Wq, L0_ffn_bq, L0_ffn_Wk, L0_ffn_bk, L0_ffn_Wv, L0_ffn_bv, L0_ffn_Wo, L0_ffn_bo, L0_ffn_Wr, L0_ffn_br, L0_ffn_e_w1, L0_ffn_e_b1, L0_ffn_e_w2, L0_ffn_e_b2)
    return x

_drawn_inputs = setup_inputs


def setup_inputs(seed=0):
    import zlib

    import numpy as np

    out = dict(_drawn_inputs(seed))
    spreads = {'L0_attn_norm_w': (1.0, 0.2),
     'L0_attn_D': (1.0, 0.2),
     'L0_xattn_bq': (0.0, 0.716),
     'L0_xattn_bk': (0.0, 2.0),
     'L0_xattn_bv': (0.0, 0.1),
     'L0_xattn_bo': (0.0, 0.1),
     'L0_ffn_ln1_g': (1.0, 0.6),
     'L0_ffn_ln1_b': (0.0, 0.8),
     'L0_ffn_ln2_g': (1.0, 0.6),
     'L0_ffn_ln2_b': (0.0, 0.785),
     'L0_ffn_bq': (0.0, 0.8),
     'L0_ffn_bk': (0.0, 2.0),
     'L0_ffn_bv': (0.0, 0.784),
     'L0_ffn_bo': (0.0, 0.341),
     'L0_ffn_br': (0.0, 0.325),
     'L0_ffn_e_b1': (0.0, 0.8),
     'L0_ffn_e_b2': (0.0, 0.371)}
    factors = {'L0_attn_A_proj_b': 8.0,
     'L0_ffn_Wq': 8.0,
     'L0_ffn_Wk': 8.0,
     'L0_ffn_Wv': 5.716,
     'L0_ffn_Wo': 3.806}
    for name, (base, spread) in spreads.items():
        noise = np.random.default_rng([zlib.crc32(name.encode()), seed]).standard_normal(out[name].shape)
        drawn = base * np.exp(spread * noise) if base else spread * noise
        out[name] = jnp.asarray(drawn.astype(out[name].dtype))
    for name, factor in factors.items():
        out[name] = (out[name] * factor).astype(out[name].dtype)
    return out
```

```python
from contextlib import ExitStack

import concourse.bass as bass
from concourse import mybir

F32 = mybir.dt.float32
F32R = mybir.dt.float32r
BF16 = mybir.dt.bfloat16
ALU = mybir.AluOpType
ACT = mybir.ActivationFunctionType
AX = mybir.AxisListType

P = 128
BANK = 512
MASKED = -1.0e30
STAGES = 4


class Line:

    def __init__(self, eng, sem):
        self.eng, self.sem, self.count, self.seen = eng, sem, 0, {}

    def done(self, instruction):
        instruction.then_inc(self.sem, 1)
        self.count += 1
        return (self.sem, self.count)

    def wait(self, *marks):
        for mark in marks:
            if mark is not None and self.seen.get(id(mark[0]), 0) < mark[1]:
                self.eng.wait_ge(mark[0], mark[1])
                self.seen[id(mark[0])] = mark[1]


class Lane:

    def __init__(self, sem):
        self.sem, self.count = sem, 0

    def done(self, instruction):
        instruction.then_inc(self.sem, 16)
        self.count += 16
        return (self.sem, self.count)


class Ring:

    def __init__(self, n):
        self.n, self.at, self.readers = n, 0, [[] for _ in range(n)]

    def take(self):
        i = self.at % self.n
        self.at += 1
        marks, self.readers[i] = self.readers[i], []
        return i, marks

    def free(self, i, *marks):
        self.readers[i] = list(marks)


def decoder_layer(nc, io, out, stages=4):
    x, ctxt = io["x"], io["ctx_1024"]
    B, T, D = x.shape
    S = ctxt.shape[1]
    DIN = io["L0_attn_A_proj_w"].shape[0]
    N = io["L0_attn_A_base"].shape[0]
    E, _, FF = io["L0_ffn_e_w1"].shape
    H = 16
    HD = D // H
    KD, KI, KF = D // P, DIN // P, FF // P
    TT = T // P
    NH2 = T // BANK
    SB = S // 2
    HG = 4
    G = H // HG
    ROWS = 4 * HD
    SCALE = float(HD) ** -0.5
    CH = B * T // BANK

    scan_bc = nc.dram_tensor("scan_bc", (B, 2 * N, T), F32, kind="Internal").ap()
    h2_store = nc.dram_tensor("h2_store", (B, KD, P, T), F32, kind="Internal").ap()

    ctx = ExitStack()
    with ctx:
        def sem(name):
            return ctx.enter_context(nc.semaphore(name))

        def sb(name, shape, dt=F32, at=ctx):
            return at.enter_context(nc.sbuf_tensor(name, shape, dt))

        pe, act = Line(nc.tensor, sem("pe_done")), Line(nc.scalar, sem("act_done"))
        dve, pool = Line(nc.vector, sem("dve_done")), Line(nc.gpsimd, sem("pool_done"))
        sync = Line(nc.sync, sem("sync_unused"))
        lanes = {}

        def lane(name):
            if name not in lanes:
                lanes[name] = Lane(sem("dma_" + name))
            return lanes[name]

        def load(name, dst, src, *marks):
            sync.wait(*marks)
            return lane(name).done(nc.sync.dma_start(dst, src))

        PS = ctx.enter_context(nc.psum_tensor("PS", [P, 8, BANK], F32))
        pairs = Ring(3)

        def pair(i):
            return PS[:, 2 * i:2 * i + 2, :].rearrange("p a b -> p (a b)")

        X = sb("X", [P, B, TT, D])
        WT = sb("WT", [P, B, TT, E])
        ident = sb("ident", [P, P])
        ident_bf = sb("ident_bf", [P, P], BF16)
        masks = sb("masks", [P, 2, P])
        masks_bf = sb("masks_bf", [P, 2, P], BF16)
        ones_row = sb("ones_row", [1, P])
        sel_sum = sb("sel_sum", [P, HG])
        half = sb("half", [P, 2 * TT])

        load("const", ident[:], io["c_ident"])
        load("const", masks[:], io["c_masks"])
        load("const", sel_sum[:], io["c_sel"])
        const_in = load("const", ones_row[:], io["c_ones"])
        x_in = [load("x%d" % b, X[:, b], x[b].rearrange("(t p) d -> p t d", p=P)) for b in range(B)]
        dve.wait(const_in)
        dve.done(nc.vector.tensor_copy(ident_bf[:], ident[:]))
        const_ready = dve.done(nc.vector.tensor_copy(masks_bf[:], masks[:]))
        half_ready = pool.done(nc.gpsimd.memset(half[:], -0.5))
        pe.wait(const_in, const_ready)
        x_ready = list(x_in)

        def barrier():
            marks = [(ln.sem, ln.count) for ln in (pe, act, dve, pool) if ln.count]
            marks += [(ln.sem, ln.count) for ln in lanes.values() if ln.count]
            for ln in (pe, act, dve, pool, sync):
                ln.wait(*marks)

        def mean_var(stats, moments, src, *marks):
            dve.wait(*marks)
            for t in range(TT):
                m = dve.done(nc.vector.bn_stats(stats[:, t, :], src(t)))
            dve.wait(m)
            for t in range(TT):
                m = dve.done(nc.vector.bn_aggr(moments[:, t, :], stats[:, t, :]))
            return m

        def rsqrt(dst, tmp, src, eps, *marks):
            dve.wait(*marks)
            m = dve.done(nc.vector.tensor_scalar(tmp, src, eps, None, ALU.add))
            pool.wait(m, half_ready)
            return pool.done(nc.gpsimd.tensor_tensor(dst, tmp, half[:, 0:TT], ALU.pow))

        def norm_scales(sc, moments, eps, inner_eps, m):
            var = moments[:, :, 1]
            m1 = rsqrt(sc[:, 0, :], sc[:, 2, :], var, eps, m)
            if inner_eps is None:
                return m1, sc[:, 0, :]
            dve.wait(m1)
            m = dve.done(nc.vector.tensor_tensor(sc[:, 3, :], sc[:, 0, :], sc[:, 0, :], ALU.mult))
            dve.wait(m)
            m = dve.done(nc.vector.tensor_tensor(sc[:, 3, :], sc[:, 3, :], var, ALU.mult))
            m = rsqrt(sc[:, 1, :], sc[:, 2, :], sc[:, 3, :], inner_eps, m)
            dve.wait(m)
            m = dve.done(nc.vector.tensor_tensor(sc[:, 1, :], sc[:, 0, :], sc[:, 1, :], ALU.mult))
            return m, sc[:, 1, :]

        def transpose_tokens(dst, src, scale, bias, *marks):
            for k in range(KD):
                i, free = pairs.take()
                pe.wait(*free, *marks)
                for t in range(TT):
                    m = nc.tensor.transpose(pair(i)[:, t * P:(t + 1) * P],
                                            src[:, t, k * P:(k + 1) * P], ident[:])
                m = pe.done(m)
                dve.wait(m)
                if scale is None:
                    m = dve.done(nc.vector.tensor_copy(dst[:, k, :], pair(i)))
                else:
                    m = dve.done(nc.vector.tensor_scalar(
                        dst[:, k, :], pair(i), scale[:, k:k + 1],
                        None if bias is None else bias[:, k:k + 1],
                        ALU.mult, ALU.bypass if bias is None else ALU.add))
                pairs.free(i, m)
            return m

        def project(dst_pair, lhs, rhs, K, width):
            for c0 in range(0, width, BANK):
                c1 = min(c0 + BANK, width)
                for k in range(K):
                    m = nc.tensor.matmul(dst_pair[:, c0:c1], lhs(k), rhs(k, c0, c1),
                                         start=(k == 0), stop=(k == K - 1))
            return m

        def scan_block(b, at, w):
            st = sb(f"st_m{b}", [P, TT, 6], at=at)
            mv = sb(f"mv_m{b}", [P, TT, 2], at=at)
            sc = sb(f"sc_m{b}", [P, 4, TT], at=at)
            xs = sb(f"xs_m{b}", [P, TT, D], at=at)
            xh = sb(f"xh_m{b}", [P, 2, D], at=at)
            xT = sb(f"xT_m{b}", [P, KD, T], at=at)
            xin = sb(f"xin{b}", [P, KI, T], at=at)
            z = sb(f"z{b}", [P, KI, T], at=at)
            th = sb(f"th{b}", [P, KI, T], at=at)
            y = sb(f"y{b}", [P, KI, T], at=at)
            bcs = sb(f"bcs{b}", [2 * N, T], at=at)
            bc = sb(f"bc{b}", [P, 2, 2, T], at=at)
            decay = sb(f"decay{b}", [P, 2, T], at=at)
            drive = sb(f"drive{b}", [P, 2, T], at=at)
            hs = sb(f"hs{b}", [P, 2, T], at=at)
            hc = sb(f"hc{b}", [P, 2, T], at=at)

            m = mean_var(st, mv, lambda t: X[:, b, t, :], x_ready[b])
            m, r12 = norm_scales(sc, mv, 1e-5, 1e-6, m)
            dve.wait(m)
            for t in range(TT):
                normed = dve.done(nc.vector.tensor_scalar(xs[:, t, :], X[:, b, t, :], mv[:, t, 0:1],
                                                          r12[:, t:t + 1], ALU.subtract, ALU.mult))
            ring = Ring(2)
            for t in range(TT):
                i, free = ring.take()
                dve.wait(*free)
                m = dve.done(nc.vector.tensor_scalar(xh[:, i, :], X[:, b, t, :], mv[:, t, 0:1],
                                                     sc[:, 0, t:t + 1], ALU.subtract, ALU.mult))
                dve.wait(m)
                m = dve.done(nc.vector.tensor_tensor(X[:, b, t, :], X[:, b, t, :], xh[:, i, :], ALU.add))
                ring.free(i, m)
            x_ready[b] = m
            m = transpose_tokens(xT, xs, w["norm"], None, normed)
            pe.wait(m)
            for c in range(2 * KI):
                i, free = pairs.take()
                pe.wait(*free)
                m = pe.done(project(pair(i), lambda k: w["in"][:, k, c * P:(c + 1) * P],
                                    lambda k, c0, c1: xT[:, k, c0:c1], KD, T))
                act.wait(m)
                dst = xin[:, c, :] if c < KI else z[:, c - KI, :]
                m = act.done(nc.scalar.activation(dst, pair(i), ACT.Silu))
                pairs.free(i, m)
                if c == KI - 1:
                    xin_ready = m
            z_ready = m
            pe.wait(xin_ready)
            i, free = pairs.take()
            pe.wait(*free)
            m = pe.done(project(pair(i)[0:2 * N], lambda k: w["bc"][:, k, :],
                                lambda k, c0, c1: xin[:, k, c0:c1], KI, T))
            dve.wait(m)
            m = dve.done(nc.vector.tensor_copy(bcs[:], pair(i)[0:2 * N]))
            pairs.free(i, m)
            stored = load("bc_store", scan_bc[b], bcs[:], m)
            for c in range(KI):
                i, free = pairs.take()
                pe.wait(*free)
                m = pe.done(project(pair(i), lambda k: w["A"][:, k, c * P:(c + 1) * P],
                                    lambda k, c0, c1: xin[:, k, c0:c1], KI, T))
                act.wait(m)
                th_ready = act.done(nc.scalar.activation(th[:, c, :], pair(i), ACT.Tanh,
                                                         bias=w["Ab_half"][:, c:c + 1], scale=0.5))
                pairs.free(i, th_ready)
            for c in range(KI):
                y_init = act.done(nc.scalar.activation(y[:, c, :], xin[:, c, :], ACT.Identity,
                                                       scale=w["Dw"][:, c:c + 1]))
            act.wait(th_ready)
            bc_ring, rd, rv, rh, rc = Ring(2), Ring(2), Ring(2), Ring(2), Ring(2)
            y_mark = [y_init] * KI
            pool.wait(xin_ready)
            for n in range(N):
                s, free = bc_ring.take()
                spread = load(f"bc{s}", bc[:, s, :, :],
                              scan_bc[b, n:n + N + 1:N, :].partition_broadcast(P), stored, *free)
                for c in range(KI):
                    i, free = rd.take()
                    act.wait(*free)
                    d_m = act.done(nc.scalar.activation(decay[:, i, :], th[:, c, :], ACT.Identity,
                                                        bias=w["abase_half"][:, n:n + 1],
                                                        scale=w["abase_half"][:, n:n + 1]))
                    j, free = rv.take()
                    pool.wait(spread, *free)
                    v_m = pool.done(nc.gpsimd.tensor_tensor(drive[:, j, :], xin[:, c, :],
                                                            bc[:, s, 0, :], ALU.mult))
                    k, free = rh.take()
                    dve.wait(d_m, v_m, *free)
                    h_m = dve.done(nc.vector.tensor_tensor_scan(hs[:, k, :], decay[:, i, :], drive[:, j, :],
                                                                0.0, ALU.mult, ALU.add))
                    rd.free(i, h_m)
                    rv.free(j, h_m)
                    g, free = rc.take()
                    dve.wait(h_m, spread, *free)
                    c_m = dve.done(nc.vector.tensor_tensor(hc[:, g, :], hs[:, k, :], bc[:, s, 1, :], ALU.mult))
                    rh.free(k, c_m)
                    pool.wait(c_m, y_mark[c])
                    y_mark[c] = pool.done(nc.gpsimd.tensor_tensor(y[:, c, :], y[:, c, :], hc[:, g, :], ALU.add))
                    rc.free(g, y_mark[c])
                bc_ring.free(s, c_m, v_m)
            for c in range(KI):
                dve.wait(y_mark[c], z_ready)
                m = dve.done(nc.vector.tensor_tensor(y[:, c, :], y[:, c, :], z[:, c, :], ALU.mult))
            pe.wait(m)
            add_projection(b, X[:, b], y, w["out"], KI, None, x_ready[b])

        def add_projection(b, dst, lhs, weight, K, bias_row, *marks):
            for t0 in range(0, TT, 4):
                i, free = pairs.take()
                pe.wait(*free)
                for t in range(t0, t0 + 4):
                    o = pair(i)[:, (t - t0) * D:(t - t0 + 1) * D]
                    for k in range(K):
                        m = nc.tensor.matmul(o, lhs[:, k, t * P:(t + 1) * P], weight[:, k, :],
                                             start=(k == 0), stop=(k == K - 1 and bias_row is None))
                    if bias_row is not None:
                        m = nc.tensor.matmul(o, ones_row[:], bias_row, start=False, stop=True)
                m = pe.done(m)
                dve.wait(m, *marks)
                dst4 = dst[:, t0:t0 + 4, :].rearrange("p t d -> p (t d)")
                m = dve.done(nc.vector.tensor_tensor(dst4, dst4, pair(i), ALU.add))
                pairs.free(i, m)
            return m

        def split_projection(dst, srcT, weight, bias, width, ready):
            pe.wait(ready)
            for c in range(KD):
                i, free = pairs.take()
                pe.wait(*free)
                m = pe.done(project(pair(i), lambda k: weight[:, k, c * P:(c + 1) * P],
                                    lambda k, c0, c1: srcT[:, k, c0:c1], KD, width))
                dve.wait(m)
                m = dve.done(nc.vector.tensor_scalar(dst[:, c, 0, 0:width], pair(i)[:, 0:width],
                                                     bias[:, c:c + 1], None, ALU.add))
                dve.wait(m)
                m = dve.done(nc.vector.scalar_tensor_tensor(
                    dst[:, c, 1, 0:width], pair(i)[:, 0:width], bias[:, c:c + 1],
                    dst[:, c, 0, 0:width].bitcast(F32), ALU.add, ALU.subtract))
                pairs.free(i, m)
            return m

        def attention(tag, at, qT, kT, kwidth, blocks, causal, v_aug, oT, ready):
            SLOTS = 2 * HG
            QW = BANK
            QT = QW // P
            qs = sb(f"qs{tag}", [ROWS + 2, SLOTS, QW], F32R, at=at)
            ks = sb(f"ks{tag}", [ROWS + 2, SLOTS, kwidth], F32R, at=at)
            mx = sb(f"mx{tag}", [P, 2, QT, HG], at=at)
            neg = sb(f"neg{tag}", [HG, 2, 2, QW], F32R, at=at)
            pt = sb(f"pt{tag}", [P, SLOTS, QW], at=at)
            raw = sb(f"raw{tag}", [P, 2, QW], at=at)
            rq = sb(f"rq{tag}", [P, QT, HG], at=at)
            rqw = sb(f"rqw{tag}", [P, QT, HG, 32], at=at)
            qslots, kslots, ptr = Ring(2), Ring(2), Ring(SLOTS // 2)
            mxr, negr, rawr, gath = Ring(2), Ring(2), Ring(2), Ring(2)
            ones_ready = dve.done(nc.vector.memset(ks[ROWS:ROWS + 2].bitcast(F32), 1.0))

            def stack(dst, src, g, parts, slot, c0, width, *marks):
                for j in range(HG):
                    c, r = (g * HG + j) * HD // P, (g * HG + j) * HD % P
                    for n, part in enumerate(parts):
                        m = load(f"stack{tag}{slot}", dst[n * HD:(n + 1) * HD, slot * HG + j, 0:width].bitcast(F32),
                                 src[r:r + HD, c, part, c0:c0 + width].bitcast(F32), *marks)
                return m

            def first_pass(g, q0, kslot, k_m):
                u, free = qslots.take()
                q_m = stack(qs, qT, g, (0, 1, 0, 1), u, q0, QW, ready, *free)
                x, free_mx = mxr.take()
                pe.wait(q_m, k_m)
                dve.wait(*free_mx)
                for t in range(QT):
                    keys = q0 + (t + 1) * P if causal else kwidth
                    per = 2 if keys <= BANK else 1
                    for j0 in range(0, HG, per):
                        i, free = pairs.take()
                        pe.wait(*free)
                        for j in range(j0, j0 + per):
                            base = (j - j0) * BANK
                            for c0 in range(0, keys, BANK):
                                c1 = min(c0 + BANK, keys)
                                diag = causal and c1 == keys
                                m = nc.tensor.matmul(pair(i)[:, base + c0:base + c1],
                                                     qs[0:ROWS, u * HG + j, t * P:(t + 1) * P],
                                                     ks[0:ROWS, kslot * HG + j, c0:c1],
                                                     start=True, stop=not diag)
                                if diag:
                                    m = nc.tensor.matmul(pair(i)[:, base + keys - P:base + keys], ident_bf[:],
                                                         masks_bf[:, 0, :], start=False, stop=True)
                        m = pe.done(m)
                        dve.wait(m)
                        src = (pair(i).rearrange("p (j k) -> p j k", j=2)[:, :, 0:keys] if per == 2
                               else pair(i)[:, 0:keys])
                        m = dve.done(nc.vector.tensor_reduce(mx[:, x, t, j0:j0 + per], src, AX.X, ALU.max))
                        pairs.free(i, m)
                i, free = pairs.take()
                pe.wait(m, *free)
                for t in range(QT):
                    p_m = nc.tensor.transpose(pair(i)[0:HG, t * P:(t + 1) * P], mx[:, x, t, :], ident[:])
                p_m = pe.done(p_m)
                mxr.free(x, p_m)
                e, free = negr.take()
                dve.wait(p_m, *free)
                m = dve.done(nc.vector.tensor_scalar(neg[:, e, 0, :], pair(i)[0:HG, 0:QW], -1.0, None, ALU.mult))
                dve.wait(m)
                m = dve.done(nc.vector.scalar_tensor_tensor(neg[:, e, 1, :], pair(i)[0:HG, 0:QW], -1.0,
                                                            neg[:, e, 0, :].bitcast(F32), ALU.mult, ALU.subtract))
                pairs.free(i, m)
                for j in range(HG):
                    for part in range(2):
                        q_m = load(f"stack{tag}{u}", qs[ROWS + part:ROWS + part + 1, u * HG + j, :].bitcast(F32),
                                   neg[j:j + 1, e, part, :].bitcast(F32), m)
                negr.free(e, q_m)
                return u, q_m

            def second_pass(g, q0, kslot, u, q_m):
                o, free = gath.take()
                gather = PS[:, 6 + o, :]
                pe.wait(ones_ready, q_m, *free)
                used = [n for n, (k0, _) in enumerate(blocks) if not causal or k0 < q0 + QW]
                for n in used:
                    k0, ksz = blocks[n]
                    a = max(k0 - q0, 0) if causal else 0
                    diag = causal and k0 >= q0
                    ready_pt = []
                    for j0 in range(0, HG, 2):
                        i, free = pairs.take()
                        pe.wait(*free)
                        for j in (j0, j0 + 1):
                            base = (j - j0) * BANK
                            m = nc.tensor.matmul(pair(i)[0:ksz, base + a:base + QW],
                                                 ks[:, kslot * HG + j, k0:k0 + ksz],
                                                 qs[:, u * HG + j, a:QW], start=True, stop=not diag)
                            if diag:
                                m = nc.tensor.matmul(pair(i)[0:ksz, base + a:base + a + P], ident_bf[:],
                                                     masks_bf[:, 1, :], start=False, stop=True)
                        m = pe.done(m)
                        k, free = ptr.take()
                        act.wait(m, *free)
                        m = act.done(nc.scalar.activation(
                            pt[0:ksz, 2 * k:2 * k + 2, a:QW],
                            pair(i).rearrange("p (j k) -> p j k", j=2)[0:ksz, :, a:QW], ACT.Exp, scale=SCALE))
                        pairs.free(i, m)
                        ready_pt.append((k, m))
                    pe.wait(*[m for _, m in ready_pt])
                    for j in range(HG):
                        m = nc.tensor.matmul(gather[32 * j:32 * j + 32, a:QW], v_aug[0:ksz, n, g * HG + j, :],
                                             pt[0:ksz, 2 * ready_pt[j // 2][0] + j % 2, a:QW],
                                             start=(n == 0), stop=(n == used[-1]))
                    m = pe.done(m)
                    for k, _ in ready_pt:
                        ptr.free(k, m)
                qslots.free(u, m)
                last = m
                v, free = rawr.take()
                act.wait(m, *free)
                r_m = act.done(nc.scalar.copy(raw[:, v, :], gather))
                gath.free(o, r_m)
                i, free = pairs.take()
                pe.wait(r_m, *free)
                for t in range(QT):
                    m = nc.tensor.matmul(pair(i)[:, t * HG:(t + 1) * HG], raw[:, v, t * P:(t + 1) * P],
                                         sel_sum[:], start=True, stop=True)
                m = pe.done(m)
                dve.wait(m)
                m = dve.done(nc.vector.reciprocal(rq[:].rearrange("p t j -> p (t j)"),
                                                  pair(i)[:, 0:QT * HG]))
                dve.wait(m)
                m = dve.done(nc.vector.tensor_copy(
                    rqw[:].rearrange("p t j r -> p (t j) r"),
                    rq[:].rearrange("p t j -> p (t j)").unsqueeze(2).to_broadcast([P, QT * HG, 32])))
                pe.wait(m)
                for t in range(QT):
                    m = nc.tensor.matmul(pair(i)[:, BANK + t * P:BANK + (t + 1) * P],
                                         rqw[:, t, :, :].rearrange("p j r -> p (j r)"), ident[:],
                                         start=True, stop=True)
                m = pe.done(m)
                dve.wait(m)
                m = dve.done(nc.vector.tensor_tensor(oT[:, g, q0:q0 + QW], raw[:, v, :],
                                                     pair(i)[:, BANK:2 * BANK], ALU.mult))
                pairs.free(i, m)
                rawr.free(v, m)
                return m, last

            units = [(g, q0) for g in range(G) for q0 in range(0, T, QW)]
            keys_of = {}

            def begin(n):
                g, q0 = units[n]
                if q0 == 0:
                    s, free = kslots.take()
                    keys_of[g] = s, stack(ks, kT, g, (0, 0, 1, 1), s, 0, kwidth, ready, *free)
                return (g, q0, keys_of[g][0], *first_pass(g, q0, *keys_of[g]))

            unit = begin(0)
            for n in range(len(units)):
                following = begin(n + 1) if n + 1 < len(units) else None
                m, last = second_pass(*unit)
                if units[n][1] == T - QW:
                    kslots.free(unit[2], last)
                unit = following
            return m

        def values(v_aug, srcT, weight, bias_row, blocks, ones_m, ready):
            pe.wait(ready)
            for n, (k0, ksz) in enumerate(blocks):
                i, free = pairs.take()
                pe.wait(*free)
                for k in range(KD):
                    nc.tensor.matmul(pair(i)[0:ksz, 0:D], srcT[:, k, k0:k0 + ksz], weight[:, k, :],
                                     start=(k == 0), stop=False)
                m = pe.done(nc.tensor.matmul(pair(i)[0:ksz, 0:D], ones_row[:, 0:ksz], bias_row,
                                             start=False, stop=True))
                dve.wait(m, ones_m)
                m = dve.done(nc.vector.tensor_copy(
                    v_aug[0:ksz, n, :, 0:HD], pair(i)[0:ksz, 0:D].rearrange("p (h d) -> p h d", d=HD)))
                pairs.free(i, m)
            return m

        def cross_block(b, at, w):
            st = sb(f"st_c{b}", [P, TT, 6], at=at)
            mv = sb(f"mv_c{b}", [P, TT, 2], at=at)
            sc = sb(f"sc_c{b}", [P, 4, TT], at=at)
            xs = sb(f"xs_c{b}", [P, TT, D], at=at)
            xT = sb(f"xT_c{b}", [P, KD, T], at=at)
            cx = sb(f"cx{b}", [SB, 2, D], at=at)
            cT = sb(f"cT{b}", [P, KD, S], at=at)
            qT = sb(f"qT_c{b}", [P, KD, 2, T], F32R, at=at)
            kT = sb(f"kT_c{b}", [P, KD, 2, S], F32R, at=at)
            va = sb(f"va_c{b}", [SB, 2, H, 32], at=at)
            oT = sb(f"oT_c{b}", [P, G, T], at=at)
            ctx_in = load("ctx", cx[:], ctxt[b].rearrange("(n p) d -> p n d", p=SB))
            ones_m = pool.done(nc.gpsimd.memset(va[:], 1.0))
            m = mean_var(st, mv, lambda t: X[:, b, t, :], x_ready[b])
            m, r1 = norm_scales(sc, mv, 1e-5, None, m)
            dve.wait(m)
            for t in range(TT):
                m = dve.done(nc.vector.tensor_scalar(xs[:, t, :], X[:, b, t, :], mv[:, t, 0:1],
                                                     r1[:, t:t + 1], ALU.subtract, ALU.mult))
            x_m = transpose_tokens(xT, xs, None, None, m)
            for k in range(KD):
                i, free = pairs.take()
                pe.wait(ctx_in, *free)
                for n in range(2):
                    m = nc.tensor.transpose(pair(i)[:, n * SB:(n + 1) * SB],
                                            cx[:, n, k * P:(k + 1) * P], ident[0:SB, 0:SB])
                m = pe.done(m)
                dve.wait(m)
                c_m = dve.done(nc.vector.tensor_copy(cT[:, k, :], pair(i)[:, 0:S]))
                pairs.free(i, c_m)
            blocks = [(0, SB), (SB, SB)]
            q_m = split_projection(qT, xT, w["xWq"], w["xbq"], T, x_m)
            k_m = split_projection(kT, cT, w["xWk"], w["xbk"], S, c_m)
            v_m = values(va, cT, w["xWv"], w["xbv"][:], blocks, ones_m, c_m)
            pe.wait(v_m)
            m = attention(f"_c{b}", at, qT, kT, S, blocks, False, va, oT, k_m)
            pe.wait(m)
            x_ready[b] = add_projection(b, X[:, b], oT, w["xWo"], G, w["xbo"][:], x_ready[b])

        def self_block(b, at, w):
            st = sb(f"st_s{b}", [P, TT, 6], at=at)
            mv = sb(f"mv_s{b}", [P, TT, 2], at=at)
            sc = sb(f"sc_s{b}", [P, 4, TT], at=at)
            A = sb(f"A{b}", [P, TT, D], at=at)
            va = sb(f"va_s{b}", [P, TT, H, 32], at=at)
            qT = sb(f"qT_s{b}", [P, KD, 2, T], F32R, at=at)
            kT = sb(f"kT_s{b}", [P, KD, 2, T], F32R, at=at)
            oT = sb(f"oT_s{b}", [P, G, T], at=at)
            ones_m = pool.done(nc.gpsimd.memset(va[:], 1.0))
            with ExitStack() as inner:
                xs = sb(f"xs_s{b}", [P, TT, D], at=inner)
                xT = sb(f"xT_s{b}", [P, KD, T], at=inner)
                m = mean_var(st, mv, lambda t: X[:, b, t, :], x_ready[b])
                m, r12 = norm_scales(sc, mv, 1e-5, 1e-5, m)
                dve.wait(m)
                for t in range(TT):
                    dve.done(nc.vector.tensor_scalar(A[:, t, :], X[:, b, t, :], mv[:, t, 0:1],
                                                     sc[:, 0, t:t + 1], ALU.subtract, ALU.mult))
                    m = dve.done(nc.vector.tensor_scalar(xs[:, t, :], X[:, b, t, :], mv[:, t, 0:1],
                                                         r12[:, t:t + 1], ALU.subtract, ALU.mult))
                x_m = transpose_tokens(xT, xs, w["g1"], w["b1"], m)
                q_m = split_projection(qT, xT, w["Wq"], w["bq"], T, x_m)
                k_m = split_projection(kT, xT, w["Wk"], w["bk"], T, x_m)
                blocks = [(n * P, P) for n in range(TT)]
                v_m = values(va, xT, w["Wv"], w["bv"][:], blocks, ones_m, x_m)
                barrier()
            with ExitStack() as inner:
                m = attention(f"_s{b}", inner, qT, kT, T, blocks, True, va, oT, k_m)
                pe.wait(m)
                m = add_projection(b, A, oT, w["Wo"], G, w["bo"][:])
                barrier()
            with ExitStack() as inner:
                xs = sb(f"xs_r{b}", [P, TT, D], at=inner)
                hT = sb(f"hT_r{b}", [P, KD, T], at=inner)
                lg = sb(f"lg{b}", [P, TT, E], at=inner)
                top = sb(f"top{b}", [P, TT, 8], at=inner)
                ex = sb(f"ex{b}", [P, TT, E], at=inner)
                keep = sb(f"keep{b}", [P, TT, E], at=inner)
                sm = sb(f"sm{b}", [P, 2, TT], at=inner)
                wT = sb(f"wT{b}", [E, T], at=inner)
                m = mean_var(st, mv, lambda t: A[:, t, :], m)
                m, r = norm_scales(sc, mv, 1e-5, None, m)
                dve.wait(m)
                for t in range(TT):
                    m = dve.done(nc.vector.tensor_scalar(xs[:, t, :], A[:, t, :], mv[:, t, 0:1],
                                                         r[:, t:t + 1], ALU.subtract, ALU.mult))
                Xb = X[:, b].rearrange("p t d -> p (t d)")
                dve.done(nc.vector.tensor_tensor(Xb, Xb, A[:].rearrange("p t d -> p (t d)"), ALU.add))
                h_m = transpose_tokens(hT, xs, w["g2"], w["b2"], m)
                for k in range(KD):
                    h2_stored[b] = load("h2_store", h2_store[b, k], hT[:, k, :], h_m)
                i, free = pairs.take()
                pe.wait(h_m, *free)
                for t in range(TT):
                    o = pair(i)[:, t * E:(t + 1) * E]
                    for k in range(KD):
                        nc.tensor.matmul(o, hT[:, k, t * P:(t + 1) * P], w["Wr"][:, k, :],
                                         start=(k == 0), stop=False)
                    m = nc.tensor.matmul(o, ones_row[:], w["br"][:], start=False, stop=True)
                m = pe.done(m)
                dve.wait(m)
                m = dve.done(nc.vector.tensor_copy(lg[:].rearrange("p t e -> p (t e)"), pair(i)[:, 0:TT * E]))
                pairs.free(i, m)
                dve.wait(m)
                for t in range(TT):
                    m = dve.done(nc.vector.max(top[:, t, :], lg[:, t, :]))
                dve.wait(m)
                dve.done(nc.vector.tensor_tensor(keep[:], lg[:], top[:, :, 1:2].to_broadcast([P, TT, E]),
                                                 ALU.is_ge))
                m = dve.done(nc.vector.tensor_tensor(lg[:], lg[:], top[:, :, 0:1].to_broadcast([P, TT, E]),
                                                     ALU.subtract))
                act.wait(m)
                m = act.done(nc.scalar.activation(ex[:], lg[:], ACT.Exp))
                dve.wait(m)
                m = dve.done(nc.vector.tensor_tensor(ex[:], ex[:], keep[:], ALU.mult))
                dve.wait(m)
                m = dve.done(nc.vector.tensor_reduce(sm[:, 0, :], ex[:], AX.X, ALU.add))
                dve.wait(m)
                m = dve.done(nc.vector.reciprocal(sm[:, 1, :], sm[:, 0, :]))
                dve.wait(m)
                m = dve.done(nc.vector.tensor_tensor(
                    WT[:, b], ex[:], sm[:, 1, :].unsqueeze(2).to_broadcast([P, TT, E]), ALU.mult))
                i, free = pairs.take()
                pe.wait(m, *free)
                for t in range(TT):
                    m = nc.tensor.transpose(pair(i)[0:E, t * P:(t + 1) * P], WT[:, b, t, :], ident[:])
                m = pe.done(m)
                dve.wait(m)
                m = dve.done(nc.vector.tensor_copy(wT[:], pair(i)[0:E]))
                pairs.free(i, m)
                pe.wait(m)
                for t0 in range(0, TT, 4):
                    i, free = pairs.take()
                    pe.wait(*free)
                    for t in range(t0, t0 + 4):
                        m = nc.tensor.matmul(pair(i)[:, (t - t0) * D:(t - t0 + 1) * D],
                                             wT[:, t * P:(t + 1) * P], w["eb2"][:], start=True, stop=True)
                    m = pe.done(m)
                    dve.wait(m)
                    dst4 = X[:, b, t0:t0 + 4, :].rearrange("p t d -> p (t d)")
                    m = dve.done(nc.vector.tensor_tensor(dst4, dst4, pair(i), ALU.add))
                    pairs.free(i, m)
                x_ready[b] = m
                barrier()

        def mixture(at):
            h2 = sb("h2", [P, KD, 2, B * T], F32R, at=at)
            w1 = sb("w1", [P, 2, KD, 2, FF], F32R, at=at)
            w2 = sb("w2", [P, 2, KF, 2, D], F32R, at=at)
            raw = sb("raw_e", [P, 2, BANK], at=at)
            eb1 = sb("eb1", [P, E, KF], at=at)
            mid = sb("mid", [P, KF, 2, BANK], F32R, at=at)
            gl = sb("gl", [P, 3, BANK], at=at)
            raws, gls, hbanks, obanks = Ring(2), Ring(3), Ring(4), Ring(2)
            act.wait(load("eb1", eb1[:], io["cols_L0_ffn_e_b1"]))

            def split(engine, ns, dst_hi, dst_lo, src, *marks):
                engine.wait(*marks)
                m = engine.done(ns.tensor_copy(dst_hi, src))
                engine.wait(m)
                return engine.done(ns.tensor_tensor(dst_lo, src, dst_hi.bitcast(F32), ALU.subtract))

            w_free = {("w1", 0): None, ("w1", 1): None, ("w2", 0): None, ("w2", 1): None}

            def expert_weights(e):
                marks = []
                W1, W2 = (io[n][e].rearrange("(k p) n -> p k n", p=P) for n in ("L0_ffn_e_w1", "L0_ffn_e_w2"))
                c1 = [(slice(k, k + 1), slice(n, n + BANK)) for k in range(KD) for n in range(0, FF, BANK)]
                c2 = [(slice(k, k + BANK // D), slice(0, D)) for k in range(0, KF, BANK // D)]
                for name, dst, src, pieces in (("w1", w1, W1, c1), ("w2", w2, W2, c2)):
                    for ks_, ns_ in pieces:
                        r, free = raws.take()
                        flat = raw[:, r, :].rearrange("p (k n) -> p k n", k=ks_.stop - ks_.start)
                        m = load(f"raw{r}", flat, src[:, ks_, ns_], *free)
                        m = split(pool, nc.gpsimd, dst[:, e % 2, ks_, 0, ns_], dst[:, e % 2, ks_, 1, ns_],
                                  flat, m, w_free[name, e % 2])
                        raws.free(r, m)
                    marks.append(m)
                return marks

            w_ready = [expert_weights(0)]
            h2_ready = []
            for b in range(B):
                for t0 in range(0, T, BANK):
                    for k in range(KD):
                        r, free = raws.take()
                        m = load(f"raw{r}", raw[:, r, :], h2_store[b, k, :, t0:t0 + BANK], h2_stored[b], *free)
                        o = slice(b * T + t0, b * T + t0 + BANK)
                        m = split(dve, nc.vector, h2[:, k, 0, o], h2[:, k, 1, o], raw[:, r, :], m)
                        raws.free(r, m)
                    h2_ready.append(m)

            mid_free = [None] * KF
            PARTS = ((0, 0), (0, 1), (1, 0))

            def up(e, c, f):
                i, free = hbanks.take()
                pe.wait(w_ready[e][0], h2_ready[c], *free)
                for k in range(KD):
                    for a, bb in PARTS:
                        m = nc.tensor.matmul(PS[:, i, :], w1[:, e % 2, k, a, f * P:(f + 1) * P],
                                             h2[:, k, bb, c * BANK:(c + 1) * BANK],
                                             start=(k == 0 and (a, bb) == (0, 0)),
                                             stop=(k == KD - 1 and (a, bb) == PARTS[-1]))
                h_m = pe.done(m)
                g, free = gls.take()
                act.wait(h_m, *free)
                m = act.done(nc.scalar.activation(gl[:, g, :], PS[:, i, :], ACT.Gelu, bias=eb1[:, e, f:f + 1]))
                hbanks.free(i, m)
                return h_m, g, m

            def down(e, c, f, o, mid_m):
                pe.wait(mid_m, w_ready[e][1])
                for t in range(BANK // P):
                    acc = PS[:, 4 + 2 * o + t // 2, (t % 2) * D:(t % 2 + 1) * D]
                    for a, bb in PARTS:
                        first = f == 0 and t % 2 == 0 and (a, bb) == (0, 0)
                        m = nc.tensor.matmul(acc, mid[:, f, a, t * P:(t + 1) * P], w2[:, e % 2, f, bb, :],
                                             start=first, stop=(f == KF - 1 and (a, bb) == PARTS[-1]),
                                             skip_group_check=True)
                return pe.done(m)

            chunks = [(e, c) for e in range(E) for c in range(CH)]
            mid_m, o_slot = {}, {}
            for n in range(len(chunks) + 1):
                for f in range(KF):
                    if n < len(chunks):
                        e, c = chunks[n]
                        h_m, g, g_m = up(e, c, f)
                    if n > 0:
                        pe_, pc = chunks[n - 1]
                        if f == 0:
                            o_slot[n - 1], free = obanks.take()
                            pe.wait(*free)
                        d_m = mid_free[f] = down(pe_, pc, f, o_slot[n - 1], mid_m[f])
                    if n < len(chunks):
                        mid_m[f] = split(dve, nc.vector, mid[:, f, 0, :], mid[:, f, 1, :], gl[:, g, :],
                                         g_m, mid_free[f])
                        gls.free(g, mid_m[f])
                if n < len(chunks) and c == CH - 1:
                    w_free["w1", e % 2] = h_m
                if n > 0:
                    e, c = chunks[n - 1]
                    b = c * BANK // T
                    dve.wait(d_m, x_ready[b])
                    for t in range(BANK // P):
                        tile = (c * BANK % T) // P + t
                        m = dve.done(nc.vector.scalar_tensor_tensor(
                            X[:, b, tile, :], PS[:, 4 + 2 * o_slot[n - 1] + t // 2, (t % 2) * D:(t % 2 + 1) * D],
                            WT[:, b, tile, e:e + 1], X[:, b, tile, :], ALU.mult, ALU.add))
                    obanks.free(o_slot[n - 1], m)
                    x_ready[b] = m
                    if c == CH - 1:
                        w_free["w2", e % 2] = d_m
                if n < len(chunks) and chunks[n][1] == 1 and chunks[n][0] + 1 < E:
                    w_ready.append(expert_weights(chunks[n][0] + 1))

        def load_weights(at, tag, table):
            w = {}
            for name, (shape, parts, zero) in table.items():
                t = w[name] = sb(f"w_{name}{tag}", shape, at=at)
                z_m = pool.done(nc.gpsimd.memset(t[:], 0.0)) if zero else None
                for dst, src in parts(t):
                    w_m = load("weights", dst, src, z_m)
            pe.wait(w_m)
            return w, w_m

        def rows(name, k):
            src = io[name]
            return ([P, k, src.shape[1]], lambda t: [(t[:], src.rearrange("(k p) n -> p k n", p=P))], False)

        def column(name, k):
            return ([P, k], lambda t: [(t[:], io["cols_" + name])], False)

        def row(name):
            return ([1, io[name].shape[0]], lambda t: [(t[:], io[name].unsqueeze(0))], False)

        def head_rows(name):
            src = io[name]
            return ([P, G, D], lambda t: [(t[32 * j:32 * j + HD, :, :],
                                           src.rearrange("(g j d) n -> j d g n", j=HG, d=HD)[j])
                                          for j in range(HG)], True)

        h2_stored = [None] * B
        mamba_table = {
            "norm": column("L0_attn_norm_w", KD), "in": rows("L0_attn_in_proj_w", KD),
            "bc": ([P, KI, 2 * N], lambda t: [
                (t[:, :, 0:N], io["L0_attn_B_proj_w"].rearrange("(k p) n -> p k n", p=P)),
                (t[:, :, N:2 * N], io["L0_attn_C_proj_w"].rearrange("(k p) n -> p k n", p=P))], False),
            "A": rows("L0_attn_A_proj_w", KI), "Ab_half": column("L0_attn_A_proj_b", KI),
            "Dw": column("L0_attn_D", KI), "out": rows("L0_attn_out_proj_w", KI),
            "abase_half": ([P, N], lambda t: [(t[:], io["L0_attn_A_base"].partition_broadcast(P))], False),
        }
        cross_table = {
            "xWq": rows("L0_xattn_Wq", KD), "xbq": column("L0_xattn_bq", KD),
            "xWk": rows("L0_xattn_Wk", KD), "xbk": column("L0_xattn_bk", KD),
            "xWv": rows("L0_xattn_Wv", KD), "xbv": row("L0_xattn_bv"),
            "xWo": head_rows("L0_xattn_Wo"), "xbo": row("L0_xattn_bo"),
        }
        self_table = {
            "g1": column("L0_ffn_ln1_g", KD), "b1": column("L0_ffn_ln1_b", KD),
            "g2": column("L0_ffn_ln2_g", KD), "b2": column("L0_ffn_ln2_b", KD),
            "Wq": rows("L0_ffn_Wq", KD), "bq": column("L0_ffn_bq", KD),
            "Wk": rows("L0_ffn_Wk", KD), "bk": column("L0_ffn_bk", KD),
            "Wv": rows("L0_ffn_Wv", KD), "bv": row("L0_ffn_bv"),
            "Wo": head_rows("L0_ffn_Wo"), "bo": row("L0_ffn_bo"),
            "Wr": rows("L0_ffn_Wr", KD), "br": row("L0_ffn_br"),
            "eb2": ([E, D], lambda t: [(t[:], io["L0_ffn_e_b2"])], False),
        }
        for b in range(B):
            with ExitStack() as at:
                w, w_m = load_weights(at, f"_m{b}", mamba_table)
                act.wait(w_m)
                m = act.done(nc.scalar.activation(w["abase_half"][:], w["abase_half"][:], ACT.Tanh, scale=0.5))
                dve.wait(m, w_m)
                m = dve.done(nc.vector.tensor_scalar(w["abase_half"][:], w["abase_half"][:], 0.25, 0.25,
                                                     ALU.mult, ALU.add))
                m = dve.done(nc.vector.tensor_scalar(w["Ab_half"][:], w["Ab_half"][:], 0.5, None, ALU.mult))
                act.wait(m)
                scan_block(b, at, w)
                barrier()
            if stages >= 2:
                with ExitStack() as at:
                    w, w_m = load_weights(at, f"_c{b}", cross_table)
                    dve.wait(w_m)
                    cross_block(b, at, w)
                    barrier()
            if stages >= 3:
                with ExitStack() as at:
                    w, w_m = load_weights(at, f"_s{b}", self_table)
                    dve.wait(w_m)
                    self_block(b, at, w)
                    barrier()
        if stages >= 4:
            with ExitStack() as at:
                mixture(at)
                barrier()
        outs = [load("out", out[b].rearrange("(t p) d -> p t d", p=P), X[:, b], x_ready[b]) for b in range(B)]
        sync.wait(outs[-1])


_COLUMNS = ["L0_attn_norm_w", "L0_attn_A_proj_b", "L0_attn_D", "L0_xattn_bq", "L0_xattn_bk",
            "L0_ffn_ln1_g", "L0_ffn_ln1_b", "L0_ffn_ln2_g", "L0_ffn_ln2_b", "L0_ffn_bq", "L0_ffn_bk"]
_OUT_SHAPE = (4, 1024, 256)


def kernel(**inputs):
    import numpy as np
    import concourse.bacc as bacc
    from concourse.bass_utils import run_bass_kernel_spmd as run

    nc = bacc.Bacc("TRN2", target_bir_lowering=False, num_devices=1)
    r = np.arange(128)
    consts = {
        "c_ident": np.eye(128, dtype=np.float32),
        "c_masks": np.stack([np.where(r[None, :] > r[:, None], MASKED, 0.0),
                             np.where(r[:, None] > r[None, :], MASKED, 0.0)], 1).astype(np.float32),
        "c_sel": (r[:, None] == 32 * np.arange(4)[None, :] + 16).astype(np.float32),
        "c_ones": np.ones((1, 128), np.float32),
    }
    columns = {"cols_" + name: np.asarray(inputs[name]).reshape(-1, 128).T for name in _COLUMNS}
    eb1 = np.asarray(inputs["L0_ffn_e_b1"])
    columns["cols_L0_ffn_e_b1"] = eb1.reshape(eb1.shape[0], -1, 128).transpose(2, 0, 1)
    arrays, io = {}, {}
    for name, value in {**inputs, **columns, **consts}.items():
        a = np.ascontiguousarray(value)
        arrays["in_" + name] = a
        io[name] = nc.dram_tensor("in_" + name, a.shape, mybir.dt.from_np(a.dtype), kind="ExternalInput").ap()
    out = nc.dram_tensor("out_x", _OUT_SHAPE, F32, kind="ExternalOutput").ap()
    decoder_layer(nc, io, out, STAGES)
    result = run(nc, [arrays], core_ids=[0])
    return result.results[0]["out_x"]
```

```python
from contextlib import ExitStack

import concourse.bass as bass
from concourse import mybir

F32 = mybir.dt.float32
F32R = mybir.dt.float32r
BF16 = mybir.dt.bfloat16
ALU = mybir.AluOpType
ACT = mybir.ActivationFunctionType
AX = mybir.AxisListType

P = 128
BANK = 512
MASKED = -1.0e30
STAGES = 4


class Stream:

    current = None

    def __init__(self):
        self.last = {}

    @staticmethod
    def note(mark):
        if Stream.current is not None:
            Stream.current.last[id(mark[0])] = mark
        return mark


def weave(*tracks):
    at = [0.0] * len(tracks)
    live = set(range(len(tracks)))
    outer = Stream.current
    while live:
        n = min(live, key=lambda k: at[k] / tracks[k][2])
        if tracks[n][0] is not None:
            Stream.current = tracks[n][0]
        step = next(tracks[n][1], None)
        if step is None:
            live.discard(n)
        else:
            at[n] += step
        Stream.current = outer
        if step is not None:
            yield step


class Line:

    def __init__(self, eng, sem):
        self.eng, self.sem, self.count, self.seen = eng, sem, 0, {}

    def done(self, instruction):
        instruction.then_inc(self.sem, 1)
        self.count += 1
        return Stream.note((self.sem, self.count))

    def wait(self, *marks):
        for mark in marks:
            if mark is not None and self.seen.get(id(mark[0]), 0) < mark[1]:
                self.eng.wait_ge(mark[0], mark[1])
                self.seen[id(mark[0])] = mark[1]


class Lane:

    def __init__(self, sem):
        self.sem, self.count = sem, 0

    def done(self, instruction):
        instruction.then_inc(self.sem, 16)
        self.count += 16
        return Stream.note((self.sem, self.count))


class Ring:

    def __init__(self, n):
        self.n, self.at, self.readers = n, 0, [[] for _ in range(n)]

    def take(self):
        i = self.at % self.n
        self.at += 1
        marks, self.readers[i] = self.readers[i], None
        assert marks is not None, "the next buffer's readers are not queued yet"
        return i, marks

    def free(self, i, *marks):
        self.readers[i] = list(marks)


def decoder_layer(nc, io, out, stages=4):
    x, ctxt = io["x"], io["ctx_1024"]
    B, T, D = x.shape
    S = ctxt.shape[1]
    DIN = io["L0_attn_A_proj_w"].shape[0]
    N = io["L0_attn_A_base"].shape[0]
    E, _, FF = io["L0_ffn_e_w1"].shape
    H = 16
    HD = D // H
    KD, KI, KF = D // P, DIN // P, FF // P
    TT = T // P
    NH2 = T // BANK
    SB = S // 2
    HG = 4
    G = H // HG
    SCALE = float(HD) ** -0.5
    CH = B * T // BANK

    scan_bc = nc.dram_tensor("scan_bc", (B, 2 * N, T), F32, kind="Internal").ap()
    x_store = nc.dram_tensor("x_store", (B, T, D), F32, kind="Internal").ap()
    stores = {name: [nc.dram_tensor(f"{name}_store{b}", (D // (HG * HD), 3, HD, HG, n), BF16, kind="Internal").ap()
                     for b in range(B)] for name, n in (("xq", T), ("xk", S), ("q", T), ("k", T))}
    h2_store = nc.dram_tensor("h2_store", (B, KD, P, T), F32, kind="Internal").ap()

    ctx = ExitStack()
    with ctx:
        def sem(name):
            return ctx.enter_context(nc.semaphore(name))

        def sb(name, shape, dt=F32, at=ctx):
            return at.enter_context(nc.sbuf_tensor(name, shape, dt))

        pe, act = Line(nc.tensor, sem("pe_done")), Line(nc.scalar, sem("act_done"))
        dve, pool = Line(nc.vector, sem("dve_done")), Line(nc.gpsimd, sem("pool_done"))
        sync = Line(nc.sync, sem("sync_unused"))
        lanes = {}

        def lane(name):
            if name not in lanes:
                lanes[name] = Lane(sem("dma_" + name))
            return lanes[name]

        def load(name, dst, src, *marks):
            sync.wait(*marks)
            return lane(name).done(nc.sync.dma_start(dst, src))

        PS = ctx.enter_context(nc.psum_tensor("PS", [P, 8, BANK], F32))
        pairs = Ring(3)

        def pair(i):
            return PS[:, 2 * i:2 * i + 2, :].rearrange("p a b -> p (a b)")

        WT = sb("WT", [P, B, TT, E])
        ident = sb("ident", [P, P])
        ident_bf = sb("ident_bf", [P, P], BF16)
        masks = sb("masks", [P, 2, P])
        masks_bf = sb("masks_bf", [P, 2, P], BF16)
        ones_row = sb("ones_row", [1, P])
        sel_sum = sb("sel_sum", [P, HG])
        half = sb("half", [P, TT])

        load("const", ident[:], io["c_ident"])
        load("const", masks[:], io["c_masks"])
        load("const", sel_sum[:], io["c_sel"])
        const_in = load("const", ones_row[:], io["c_ones"])
        dve.wait(const_in)
        dve.done(nc.vector.tensor_copy(ident_bf[:], ident[:]))
        const_ready = dve.done(nc.vector.tensor_copy(masks_bf[:], masks[:]))
        gather_clear = dve.done(nc.vector.memset(PS[:, 6:8, :], 0.0))
        half_ready = pool.done(nc.gpsimd.memset(half[:], -0.5))
        pe.wait(const_in, const_ready, gather_clear)

        def settle(*more):
            for ln in (pe, act, dve, pool, sync):
                ln.wait(*Stream.current.last.values(), *more)

        def mean_var(stats, moments, src, *marks):
            dve.wait(*marks)
            for t in range(TT):
                m = dve.done(nc.vector.bn_stats(stats[:, t, :], src(t)))
            dve.wait(m)
            for t in range(TT):
                m = dve.done(nc.vector.bn_aggr(moments[:, t, :], stats[:, t, :]))
            return m

        def rsqrt(dst, tmp, src, eps, *marks):
            dve.wait(*marks)
            m = dve.done(nc.vector.tensor_scalar(tmp, src, eps, None, ALU.add))
            pool.wait(m, half_ready)
            return pool.done(nc.gpsimd.tensor_tensor(dst, tmp, half[:, 0:TT], ALU.pow))

        def norm_scales(sc, moments, eps, inner_eps, m):
            var = moments[:, :, 1]
            m1 = rsqrt(sc[:, 0, :], sc[:, 2, :], var, eps, m)
            if inner_eps is None:
                return m1, sc[:, 0, :]
            dve.wait(m1)
            m = dve.done(nc.vector.tensor_tensor(sc[:, 3, :], sc[:, 0, :], sc[:, 0, :], ALU.mult))
            dve.wait(m)
            m = dve.done(nc.vector.tensor_tensor(sc[:, 3, :], sc[:, 3, :], var, ALU.mult))
            m = rsqrt(sc[:, 1, :], sc[:, 2, :], sc[:, 3, :], inner_eps, m)
            dve.wait(m)
            m = dve.done(nc.vector.tensor_tensor(sc[:, 1, :], sc[:, 0, :], sc[:, 1, :], ALU.mult))
            return m, sc[:, 1, :]

        def normed(dst, b_t, moments, t, scale):
            return dve.done(nc.vector.tensor_scalar(dst, b_t, moments[:, t, 0:1], scale[:, t:t + 1],
                                                    ALU.subtract, ALU.mult))

        def transpose_tokens(dst, src, scale, bias, *marks):
            for k in range(KD):
                i, free = pairs.take()
                pe.wait(*free, *marks)
                for t in range(TT):
                    m = nc.tensor.transpose(pair(i)[:, t * P:(t + 1) * P],
                                            src[:, t, k * P:(k + 1) * P], ident[:])
                m = pe.done(m)
                dve.wait(m)
                if scale is None:
                    m = dve.done(nc.vector.tensor_copy(dst[:, k, :], pair(i)))
                else:
                    m = dve.done(nc.vector.tensor_scalar(dst[:, k, :], pair(i), scale[:, k:k + 1],
                                                         bias[:, k:k + 1], ALU.mult, ALU.add))
                pairs.free(i, m)
            return m

        def project(dst_pair, lhs, rhs, K, width):
            for c0 in range(0, width, BANK):
                c1 = min(c0 + BANK, width)
                for k in range(K):
                    m = nc.tensor.matmul(dst_pair[:, c0:c1], lhs(k), rhs(k, c0, c1),
                                         start=(k == 0), stop=(k == K - 1))
            return m

        TQ = T // 4
        QTT = TQ // P
        fr = ExitStack()
        fr.__enter__()

        def fb(name, shape, dt=F32):
            return sb(name, shape, dt, at=fr)

        X = fb("X", [P, 2, TT, D])
        m_st, m_mv, m_sc = fb("m_st", [P, TT, 6]), fb("m_mv", [P, TT, 2]), fb("m_sc", [P, 4, TT])
        m_xs, m_xT = fb("m_xs", [P, QTT, D]), fb("m_xT", [P, KD, TQ])
        xh = fb("xh", [P, D])
        xin, z, th, y = (fb(n, [P, KI, TQ]) for n in ("xin", "z", "th", "y"))
        bcs = fb("bcs", [2 * N, TQ])
        bc = fb("bc", [P, 3, 2, TQ])
        decay = fb("decay", [P, 2, KI, TQ])
        drive = fb("drive", [P, 3, KI, TQ])
        state = fb("state", [P, N, KI])
        bc_ring, rd, rv = Ring(3), Ring(2), Ring(3)
        x_ready = [None] * B
        x_slot_free = [None, None]

        def flat(t):
            return t.rearrange("p a b -> p (a b)")

        def scan_block(b, w):
            xb = X[:, b % 2]
            settle()
            x_ready[b] = load(f"x{b % 2}", xb, x[b].rearrange("(t p) d -> p t d", p=P), x_slot_free[b % 2])
            m = mean_var(m_st, m_mv, lambda t: xb[:, t, :], x_ready[b])
            sc_m, r12 = norm_scales(m_sc, m_mv, 1e-5, 1e-6, m)
            yield 3
            for q in range(T // TQ):
                dve.wait(sc_m)
                for t in range(QTT):
                    m = normed(m_xs[:, t, :], xb[:, q * QTT + t, :], m_mv, q * QTT + t, r12)
                xs_m = m
                for t in range(q * QTT, (q + 1) * QTT):
                    m = normed(xh[:], xb[:, t, :], m_mv, t, m_sc[:, 0, :])
                    dve.wait(m)
                    m = dve.done(nc.vector.tensor_tensor(xb[:, t, :], xb[:, t, :], xh[:], ALU.add))
                    dve.wait(m)
                x_ready[b] = m
                i, free = pairs.take()
                pe.wait(*free, xs_m)
                for k in range(KD):
                    for t in range(QTT):
                        m = nc.tensor.transpose(pair(i)[:, k * BANK + t * P:k * BANK + (t + 1) * P],
                                                m_xs[:, t, k * P:(k + 1) * P], ident[:])
                m = pe.done(m)
                act.wait(m)
                for k in range(KD):
                    m = act.done(nc.scalar.activation(m_xT[:, k, :], pair(i)[:, k * BANK:k * BANK + TQ],
                                                      ACT.Identity, scale=w["norm"][:, k:k + 1]))
                pairs.free(i, m)
                pe.wait(m)
                yield 2
                for part, dst in ((0, xin), (1, z)):
                    i, free = pairs.take()
                    pe.wait(*free)
                    for c in range(KI):
                        m = project(pair(i)[:, c * TQ:(c + 1) * TQ],
                                    lambda k: w["in"][:, k, part * DIN + c * P:part * DIN + (c + 1) * P],
                                    lambda k, c0, c1: m_xT[:, k, c0:c1], KD, TQ)
                    m = pe.done(m)
                    act.wait(m)
                    m = act.done(nc.scalar.activation(flat(dst[:]), pair(i), ACT.Silu))
                    pairs.free(i, m)
                    if part == 0:
                        xin_ready = m
                    yield 4
                z_ready = m
                pe.wait(xin_ready)
                i, free = pairs.take()
                pe.wait(*free)
                m = pe.done(project(pair(i)[0:2 * N, 0:TQ], lambda k: w["bc"][:, k, :],
                                    lambda k, c0, c1: xin[:, k, c0:c1], KI, TQ))
                act.wait(m)
                m = act.done(nc.scalar.copy(bcs[:], pair(i)[0:2 * N, 0:TQ]))
                pairs.free(i, m)
                cols = slice(q * TQ, (q + 1) * TQ)
                stored = load("bc_store", scan_bc[b, :, cols], bcs[:], m)
                yield 2
                i, free = pairs.take()
                pe.wait(*free)
                for c in range(KI):
                    m = project(pair(i)[:, c * TQ:(c + 1) * TQ], lambda k: w["A"][:, k, c * P:(c + 1) * P],
                                lambda k, c0, c1: xin[:, k, c0:c1], KI, TQ)
                m = pe.done(m)
                act.wait(m)
                for c in range(KI):
                    th_ready = act.done(nc.scalar.activation(th[:, c, :], pair(i)[:, c * TQ:(c + 1) * TQ],
                                                             ACT.Tanh, bias=w["Ab_half"][:, c:c + 1], scale=0.5))
                pairs.free(i, th_ready)
                for c in range(KI):
                    y_mark = act.done(nc.scalar.activation(y[:, c, :], xin[:, c, :], ACT.Identity,
                                                           scale=w["Dw"][:, c:c + 1]))
                act.wait(th_ready)
                pool.wait(xin_ready)
                yield 3
                made, held = {}, {}

                def inputs_of(n):
                    s, free = bc_ring.take()
                    spread = load(f"bc{s}", bc[:, s, :, :],
                                  scan_bc[b, n:n + N + 1:N, cols].partition_broadcast(P), stored, *free)
                    i, free = rd.take()
                    act.wait(*free)
                    d_m = act.done(nc.scalar.activation(flat(decay[:, i]), flat(th[:]), ACT.Identity,
                                                        bias=w["abase_half"][:, n:n + 1],
                                                        scale=w["abase_half"][:, n:n + 1]))
                    j, free = rv.take()
                    pool.wait(spread, *free)
                    v_m = pool.done(nc.gpsimd.tensor_tensor(
                        drive[:, j], xin[:], bc[:, s, 0:1, :].to_broadcast([P, KI, TQ]), ALU.mult))
                    made[n] = s, spread, i, d_m, j, v_m

                def add_to_y(n):
                    nonlocal y_mark
                    g, c_m = held.pop(n)
                    pool.wait(c_m, y_mark)
                    y_mark = pool.done(nc.gpsimd.tensor_tensor(flat(y[:]), flat(y[:]), flat(drive[:, g]), ALU.add))
                    rv.free(g, y_mark)

                inputs_of(0)
                for n in range(N):
                    if n + 1 < N:
                        inputs_of(n + 1)
                    s, spread, i, d_m, j, v_m = made.pop(n)
                    dve.wait(d_m, v_m)
                    for c in range(KI):
                        h_m = dve.done(nc.vector.tensor_tensor_scan(
                            drive[:, j, c, :], decay[:, i, c, :], drive[:, j, c, :],
                            0.0 if q == 0 else state[:, n, c:c + 1], ALU.mult, ALU.add))
                    rd.free(i, h_m)
                    dve.wait(h_m, spread)
                    s_m = dve.done(nc.vector.tensor_copy(state[:, n, :], drive[:, j, :, TQ - 1]))
                    dve.wait(s_m)
                    c_m = dve.done(nc.vector.tensor_tensor(
                        drive[:, j], drive[:, j], bc[:, s, 1:2, :].to_broadcast([P, KI, TQ]), ALU.mult))
                    held[n] = j, c_m
                    bc_ring.free(s, c_m, v_m)
                    if n > 0:
                        add_to_y(n - 1)
                    yield 5
                dve.wait(s_m)
                add_to_y(N - 1)
                dve.wait(y_mark, z_ready)
                m = dve.done(nc.vector.tensor_tensor(flat(y[:]), flat(y[:]), flat(z[:]), ALU.mult))
                i, free = pairs.take()
                pe.wait(*free, m)
                for t in range(QTT):
                    for k in range(KI):
                        m = nc.tensor.matmul(pair(i)[:, t * D:(t + 1) * D], y[:, k, t * P:(t + 1) * P],
                                             w["out"][:, k, :], start=(k == 0), stop=(k == KI - 1))
                m = pe.done(m)
                act.wait(m)
                dst = flat(xb[:, q * QTT:(q + 1) * QTT, :])
                dve.wait(m, x_ready[b])
                m = dve.done(nc.vector.tensor_tensor(dst, dst, pair(i)[:, 0:QTT * D], ALU.add))
                x_ready[b] = m
                pairs.free(i, m)
                act.wait(m)
                yield 3

        STACK = (((0, 1, 2), 0), ((0, 1), 1), ((0,), 2))
        ROWS = 6 * HD
        QW = BANK
        QT = QW // P
        A = fb("A", [P, TT, D])
        xs, xT = fb("xs", [P, TT, D]), fb("xT", [P, KD, T])
        st, mv, sc = fb("st", [P, TT, 6]), fb("mv", [P, TT, 2]), fb("sc", [P, 4, TT])
        va = fb("va", [P, TT, H, HD + 1])
        parts, rest = fb("parts", [P, 2, 3, T], BF16), fb("rest", [P, T])
        qs = fb("qs", [ROWS + 3, 3, HG, QW], BF16)
        ks = fb("ks", [ROWS + 3, 2, HG, T], BF16)
        mx, mx_rest = fb("mx", [P, 2, QT, HG]), fb("mx_rest", [P, QT, HG])
        neg = fb("neg", [P, 2, QT, HG, 3], BF16)
        pt = fb("pt", [P, 4, 2, QW])
        raw = fb("raw", [P, 2, QW])
        rq, rqw = fb("rq", [P, QT, HG]), fb("rqw", [P, QT, HG, 32])
        oT = fb("oT", [P, 2, QW])
        qslots, kslots, ptr, partr, restr = Ring(3), Ring(2), Ring(4), Ring(2), Ring(1)
        mxr, negr, rawr, gath, oTr = Ring(2), Ring(2), Ring(2), Ring(2), Ring(2)
        ones_ready = None
        ones_ready = dve.done(nc.vector.memset(ks[ROWS:ROWS + 3], 1.0))
        va_ready = pool.done(nc.gpsimd.memset(va[:], 1.0))

        def split_projection(name, store, srcT, weight, bias, width, ready):
            pe.wait(ready)
            for c in range(KD):
                i, free = pairs.take()
                pe.wait(*free)
                m = pe.done(project(pair(i), lambda k: weight[:, k, c * P:(c + 1) * P],
                                    lambda k, c0, c1: srcT[:, k, c0:c1], KD, width))
                s, free = partr.take()
                act.wait(m, *free)
                p0, p1, p2 = (parts[:, s, r, 0:width] for r in range(3))
                m = act.done(nc.scalar.activation(p0, pair(i)[:, 0:width], ACT.Identity,
                                                  bias=bias[:, c:c + 1]))
                _, free = restr.take()
                dve.wait(m, *free)
                r_m = dve.done(nc.vector.scalar_tensor_tensor(
                    rest[:, 0:width], pair(i)[:, 0:width], bias[:, c:c + 1], p0, ALU.add, ALU.subtract))
                pairs.free(i, r_m)
                act.wait(r_m)
                m = act.done(nc.scalar.copy(p1, rest[:, 0:width]))
                dve.wait(m)
                split = dve.done(nc.vector.tensor_tensor(p2, rest[:, 0:width], p1, ALU.subtract))
                restr.free(0, split)
                rows_of = HG * HD
                for g in range(P // rows_of):
                    for r in range(3):
                        m = load(f"{name}_parts{s}", store[c * (P // rows_of) + g, r].rearrange("d j n -> j d n"),
                                 parts[g * rows_of:(g + 1) * rows_of, s, r, 0:width], split)
                partr.free(s, m)
                yield m

        def attention(q_store, k_store, kwidth, blocks, causal, stored, weight, bias_row, dst, dst_m):

            def stack(lane_name, to, source, *marks):
                row = 0
                sync.wait(*marks)
                for term in STACK:
                    n = len(term[0])
                    m = load(lane_name, to[row:row + n * HD], source(term))
                    row += n * HD
                return m

            def fetch_keys(g):
                s, free = kslots.take()
                return s, stack(f"ks{s}", ks[:, s, :, 0:kwidth],
                                lambda term: k_store[g, term[1]:term[1] + 1].rearrange("r d j n -> r d (j n)")
                                .to_broadcast([len(term[0]), HD, HG * kwidth]), *stored, *free)

            def fetch_queries(g, q0):
                u, free = qslots.take()
                return u, stack(f"qs{u}", qs[:, u],
                                lambda term: q_store[g, 0:len(term[0]), :, :, q0:q0 + QW]
                                .rearrange("r d j n -> (r d) j n"), *stored, *free)

            def head(t, slot, j, rows):
                return t[0:rows, slot, j, :]

            def first_pass(g, q0, kslot, k_m, u, q_m, result):
                x_, free_mx = mxr.take()
                pe.wait(q_m, k_m)
                dve.wait(*free_mx)
                for t in range(QT):
                    keys = q0 + (t + 1) * P if causal else kwidth
                    per = 4 if keys <= BANK // 2 else 2 if keys <= BANK else 1
                    for j0 in range(0, HG, per):
                        i, free = pairs.take()
                        pe.wait(*free)
                        for j in range(j0, j0 + per):
                            base = (0 if per == 1 else (j % 2) * BANK + (j - j0) // 2 * (BANK // 2))
                            for c0 in range(0, keys, BANK):
                                c1 = min(c0 + BANK, keys)
                                diag = causal and c1 == keys
                                m = nc.tensor.matmul(pair(i)[:, base + c0:base + c1],
                                                     head(qs, u, j, ROWS)[:, t * P:(t + 1) * P],
                                                     head(ks, kslot, j, ROWS)[:, c0:c1],
                                                     start=True, stop=not diag)
                                if diag:
                                    m = nc.tensor.matmul(pair(i)[:, base + keys - P:base + keys], ident_bf[:],
                                                         masks_bf[:, 0, :], start=False, stop=True)
                        m = pe.done(m)
                        dve.wait(m)
                        src = pair(i)
                        if per == 4:
                            src = src.rearrange("p (b a k) -> p a b k", b=2, a=2)[:, :, :, 0:keys]
                        elif per == 2:
                            src = src.rearrange("p (j k) -> p j k", j=2)[:, :, 0:keys]
                        else:
                            src = src[:, 0:keys]
                        m = dve.done(nc.vector.tensor_reduce(mx[:, x_, t, j0:j0 + per], src, AX.X, ALU.max))
                        pairs.free(i, m)
                        yield per * keys / 500
                v, free = negr.take()
                dve.wait(m, *free)
                m = dve.done(nc.vector.tensor_scalar(neg[:, v, :, :, 0], mx[:, x_], -1.0, None, ALU.mult))
                dve.wait(m)
                m = dve.done(nc.vector.scalar_tensor_tensor(mx_rest[:], mx[:, x_], -1.0, neg[:, v, :, :, 0],
                                                            ALU.mult, ALU.subtract))
                dve.wait(m)
                mxr.free(x_, m)
                m = dve.done(nc.vector.tensor_copy(neg[:, v, :, :, 1], mx_rest[:]))
                dve.wait(m)
                m = dve.done(nc.vector.tensor_tensor(neg[:, v, :, :, 2], mx_rest[:], neg[:, v, :, :, 1],
                                                     ALU.subtract))
                for j0 in range(0, HG, 2):
                    i, free = pairs.take()
                    pe.wait(m, *free)
                    for j in (j0, j0 + 1):
                        for t in range(QT):
                            c0 = (j - j0) * BANK + t * P
                            p_m = nc.tensor.matmul(pair(i)[ROWS:ROWS + 3, c0:c0 + P], neg[:, v, t, j, :],
                                                   ident_bf[:], start=True, stop=True)
                    p_m = pe.done(p_m)
                    act.wait(p_m)
                    q_m = act.done(nc.scalar.copy(qs[ROWS:ROWS + 3, u, j0:j0 + 2, :],
                                                  pair(i)[ROWS:ROWS + 3].rearrange("p (j k) -> p j k", j=2)))
                    pairs.free(i, q_m)
                negr.free(v, p_m)
                result.append((u, q_m))
                yield 1

            def second_pass(g, q0, kslot, u, q_m, result):
                o, free = gath.take()
                gather = PS[:, 6 + o, :]
                pe.wait(ones_ready, q_m, *free)
                used = [n for n, (k0, _) in enumerate(blocks) if not causal or k0 < q0 + QW]

                def gather_values(n, a, ready_pt):
                    ksz = blocks[n][1]
                    pe.wait(*[m for _, m in ready_pt])
                    for j in range(HG):
                        m = nc.tensor.matmul(gather[32 * j:32 * j + HD + 1, a:QW], va[0:ksz, n, g * HG + j, :],
                                             pt[0:ksz, ready_pt[j // 2][0], j % 2, a:QW],
                                             start=(n == 0), stop=(n == used[-1]))
                    m = pe.done(m)
                    for k, _ in ready_pt:
                        ptr.free(k, m)
                    return m

                behind = None
                for n in used:
                    k0, ksz = blocks[n]
                    a = max(k0 - q0, 0) if causal else 0
                    diag = causal and k0 >= q0
                    ready_pt = []
                    for j0 in range(0, HG, 2):
                        i, free = pairs.take()
                        pe.wait(*free)
                        for j in (j0, j0 + 1):
                            base = (j - j0) * BANK
                            m = nc.tensor.matmul(pair(i)[0:ksz, base + a:base + QW],
                                                 head(ks, kslot, j, ROWS + 2)[:, k0:k0 + ksz],
                                                 head(qs, u, j, ROWS + 2)[:, a:QW], start=True, stop=not diag)
                            if diag:
                                m = nc.tensor.matmul(pair(i)[0:ksz, base + a:base + a + P], ident_bf[:],
                                                     masks_bf[:, 1, :], start=False, stop=True)
                        m = pe.done(m)
                        k, free = ptr.take()
                        act.wait(m, *free)
                        m = act.done(nc.scalar.activation(
                            pt[0:ksz, k, :, a:QW],
                            pair(i).rearrange("p (j k) -> p j k", j=2)[0:ksz, :, a:QW], ACT.Exp, scale=SCALE))
                        pairs.free(i, m)
                        ready_pt.append((k, m))
                    if behind is not None:
                        gather_values(*behind)
                    behind = (n, a, ready_pt)
                    yield 4 * (QW - a) / 500
                m = gather_values(*behind)
                qslots.free(u, m)
                last = m
                v, free = rawr.take()
                act.wait(m, *free)
                r_m = act.done(nc.scalar.copy(raw[:, v, :], gather))
                gath.free(o, r_m)
                yield 1
                i, free = pairs.take()
                pe.wait(r_m, *free)
                for t in range(QT):
                    m = nc.tensor.matmul(pair(i)[:, t * HG:(t + 1) * HG], raw[:, v, t * P:(t + 1) * P],
                                         sel_sum[:], start=True, stop=True)
                m = pe.done(m)
                dve.wait(m)
                m = dve.done(nc.vector.reciprocal(rq[:].rearrange("p t j -> p (t j)"),
                                                  pair(i)[:, 0:QT * HG]))
                dve.wait(m)
                w_m = dve.done(nc.vector.tensor_copy(
                    rqw[:].rearrange("p t j r -> p (t j) r"),
                    rq[:].rearrange("p t j -> p (t j)").unsqueeze(2).to_broadcast([P, QT * HG, 32])))
                pairs.free(i, w_m)
                yield 1
                i, free = pairs.take()
                pe.wait(w_m, *free)
                for t in range(QT):
                    m = nc.tensor.matmul(pair(i)[:, t * P:(t + 1) * P],
                                         rqw[:, t, :, :].rearrange("p j r -> p (j r)"), ident[:],
                                         start=True, stop=True)
                m = pe.done(m)
                e, free = oTr.take()
                dve.wait(m, *free)
                m = dve.done(nc.vector.tensor_tensor(oT[:, e, :], raw[:, v, :], pair(i)[:, 0:QW], ALU.mult))
                pairs.free(i, m)
                rawr.free(v, m)
                yield 1
                i, free = pairs.take()
                pe.wait(m, *free)
                for t in range(QT):
                    p_o = pair(i)[:, t * D:(t + 1) * D]
                    m = nc.tensor.matmul(p_o, oT[:, e, t * P:(t + 1) * P], weight[:, g, :],
                                         start=True, stop=g > 0)
                    if g == 0:
                        m = nc.tensor.matmul(p_o, ones_row[:], bias_row, start=False, stop=True)
                m = pe.done(m)
                oTr.free(e, m)
                part = flat(dst[:, q0 // P:q0 // P + QT, :])
                dve.wait(m, dst_m[q0 // QW])
                dst_m[q0 // QW] = m = dve.done(nc.vector.tensor_tensor(part, part, pair(i), ALU.add))
                pairs.free(i, m)
                result.append(last)
                yield 1

            units = [(g, q0) for g in range(G) for q0 in range(0, T, QW)]
            fetched, keys_of, got = {}, {}, {}

            def fetch(n):
                if n < len(units):
                    g, q0 = units[n]
                    if q0 == 0:
                        keys_of[g] = fetch_keys(g)
                    fetched[n] = fetch_queries(g, q0)

            def start(n, result):
                g, q0 = units[n]
                return first_pass(g, q0, *keys_of[g], *fetched.pop(n), result)

            fetch(0)
            fetch(1)
            got = []
            yield from start(0, got)
            for n in range(len(units)):
                g, q0 = units[n]
                fetch(n + 2)
                nxt, done = [], []
                second = second_pass(g, q0, keys_of[g][0], *got[0], done)
                tracks = [(None, second, 1.0)]
                if n + 1 < len(units):
                    tracks.append((None, start(n + 1, nxt), 1.0))
                yield from weave(*tracks)
                if q0 == T - QW:
                    kslots.free(keys_of[g][0], done[0])
                got = nxt

        def values(srcT, weight, bias_row, blocks, ready):
            pe.wait(ready)
            for n, (k0, ksz) in enumerate(blocks):
                i, free = pairs.take()
                pe.wait(*free)
                for k in range(KD):
                    nc.tensor.matmul(pair(i)[0:ksz, 0:D], srcT[:, k, k0:k0 + ksz], weight[:, k, :],
                                     start=(k == 0), stop=False)
                m = pe.done(nc.tensor.matmul(pair(i)[0:ksz, 0:D], ones_row[:, 0:ksz], bias_row,
                                             start=False, stop=True))
                act.wait(m, va_ready)
                m = act.done(nc.scalar.copy(
                    va[0:ksz, n, :, 0:HD], pair(i)[0:ksz, 0:D].rearrange("p (h d) -> p h d", d=HD)))
                pairs.free(i, m)
                pe.wait(m) if n == len(blocks) - 1 else None
                yield 1

        cx = flat(raw[:])[0:SB, 0:2 * D].rearrange("p (n d) -> p n d", n=2)
        cT = flat(A[:])[:, 0:KD * S].rearrange("p (k s) -> p k s", k=KD)

        def cross_block(b):
            xb = X[:, b % 2]
            settle()
            w, w_m = load_weights(cross_table, w_room[:])
            ctx_in = load("ctx", cx, ctxt[b].rearrange("(n p) d -> p n d", p=SB))
            m = mean_var(st, mv, lambda t: xb[:, t, :], x_ready[b])
            m, r1 = norm_scales(sc, mv, 1e-5, None, m)
            yield 3
            dve.wait(m)
            for t in range(TT):
                m = normed(xs[:, t, :], xb[:, t, :], mv, t, r1)
            x_m = transpose_tokens(xT, xs, None, None, m)
            yield 4
            i, free = pairs.take()
            pe.wait(ctx_in, *free)
            for k in range(KD):
                for n in range(2):
                    m = nc.tensor.transpose(pair(i)[:, k * BANK + n * SB:k * BANK + (n + 1) * SB],
                                            cx[:, n, k * P:(k + 1) * P], ident[0:SB, 0:SB])
            m = pe.done(m)
            act.wait(m)
            c_m = act.done(nc.scalar.copy(cT, pair(i).rearrange("p (k s) -> p k s", k=2)[:, :, 0:S]))
            pairs.free(i, c_m)
            blocks = [(0, SB), (SB, SB)]
            for ln in (pe, act, dve):
                ln.wait(w_m)
            stored = []
            for m in split_projection("xk", stores["xk"][b], cT, w["xWk"], w["xbk"], S, c_m):
                stored.append(m)
                yield 1
            for m in split_projection("xq", stores["xq"][b], xT, w["xWq"], w["xbq"], T, x_m):
                stored.append(m)
                yield 3
            yield from values(cT, w["xWv"], w["xbv"], blocks, c_m)
            yield from attention(stores["xq"][b], stores["xk"][b], S, blocks, False, stored, w["xWo"], w["xbo"], xb, [x_ready[b], x_ready[b]])

        lg, top, ex, keep = (fb(n, [P, TT, e]) for n, e in (("lg", E), ("top", 8), ("ex", E), ("keep", E)))
        sm = fb("sm", [P, 2, TT])

        def self_block(b):
            xb = X[:, b % 2]
            settle()
            w, w_m = load_weights(self_table, w_room[:])
            m = mean_var(st, mv, lambda t: xb[:, t, :])
            m, r12 = norm_scales(sc, mv, 1e-5, 1e-5, m)
            yield 3
            dve.wait(m)
            for t in range(TT):
                normed(A[:, t, :], xb[:, t, :], mv, t, sc[:, 0, :])
                m = normed(xs[:, t, :], xb[:, t, :], mv, t, r12)
            for ln in (pe, act, dve):
                ln.wait(w_m)
            x_m = transpose_tokens(xT, xs, w["g1"], w["b1"], m)
            yield 5
            stored = []
            for m in split_projection("k", stores["k"][b], xT, w["Wk"], w["bk"], T, x_m):
                stored.append(m)
                yield 3
            for m in split_projection("q", stores["q"][b], xT, w["Wq"], w["bq"], T, x_m):
                stored.append(m)
                yield 3
            blocks = [(n * P, P) for n in range(TT)]
            yield from values(xT, w["Wv"], w["bv"], blocks, x_m)
            a_ready = [None, None]
            yield from attention(stores["q"][b], stores["k"][b], T, blocks, True, stored, w["Wo"], w["bo"], A, a_ready)
            m = mean_var(st, mv, lambda t: A[:, t, :], *a_ready)
            m, r = norm_scales(sc, mv, 1e-5, None, m)
            yield 3
            dve.wait(m)
            for t in range(TT):
                m = normed(xs[:, t, :], A[:, t, :], mv, t, r)
            base_m = dve.done(nc.vector.tensor_tensor(flat(xb), flat(xb), flat(A[:]), ALU.add))
            h_m = transpose_tokens(xT, xs, w["g2"], w["b2"], m)
            for k in range(KD):
                h2_stored[b] = load("h2_store", h2_store[b, k], xT[:, k, :], h_m)
            yield 5
            i, free = pairs.take()
            pe.wait(h_m, *free)
            for t in range(TT):
                o = pair(i)[:, t * E:(t + 1) * E]
                for k in range(KD):
                    nc.tensor.matmul(o, xT[:, k, t * P:(t + 1) * P], w["Wr"][:, k, :],
                                     start=(k == 0), stop=False)
                m = nc.tensor.matmul(o, ones_row[:], w["br"], start=False, stop=True)
            m = pe.done(m)
            dve.wait(m)
            m = dve.done(nc.vector.tensor_copy(flat(lg[:]), pair(i)[:, 0:TT * E]))
            pairs.free(i, m)
            dve.wait(m)
            for t in range(TT):
                m = dve.done(nc.vector.max(top[:, t, :], lg[:, t, :]))
            dve.wait(m)
            dve.done(nc.vector.tensor_tensor(keep[:], lg[:], top[:, :, 1:2].to_broadcast([P, TT, E]),
                                             ALU.is_ge))
            m = dve.done(nc.vector.tensor_tensor(lg[:], lg[:], top[:, :, 0:1].to_broadcast([P, TT, E]),
                                                 ALU.subtract))
            act.wait(m)
            m = act.done(nc.scalar.activation(ex[:], lg[:], ACT.Exp))
            dve.wait(m)
            m = dve.done(nc.vector.tensor_tensor(ex[:], ex[:], keep[:], ALU.mult))
            dve.wait(m)
            m = dve.done(nc.vector.tensor_reduce(sm[:, 0, :], ex[:], AX.X, ALU.add))
            dve.wait(m)
            m = dve.done(nc.vector.reciprocal(sm[:, 1, :], sm[:, 0, :]))
            dve.wait(m)
            m = dve.done(nc.vector.tensor_tensor(
                WT[:, b], ex[:], sm[:, 1, :].unsqueeze(2).to_broadcast([P, TT, E]), ALU.mult))
            yield 4
            i, free = pairs.take()
            pe.wait(m, *free)
            for t in range(TT):
                m = nc.tensor.transpose(pair(i)[0:E, t * P:(t + 1) * P], WT[:, b, t, :], ident[:])
            m = pe.done(m)
            wT = flat(xs[0:E, 0:T // D, :])
            dve.wait(m)
            m = dve.done(nc.vector.tensor_copy(wT, pair(i)[0:E]))
            pairs.free(i, m)
            pe.wait(m)
            for t0 in range(0, TT, 4):
                i, free = pairs.take()
                pe.wait(*free)
                for t in range(t0, t0 + 4):
                    m = nc.tensor.matmul(pair(i)[:, (t - t0) * D:(t - t0 + 1) * D],
                                         wT[:, t * P:(t + 1) * P], w["eb2"], start=True, stop=True)
                m = pe.done(m)
                dve.wait(m, base_m)
                dst4 = flat(xb[:, t0:t0 + 4, :])
                m = dve.done(nc.vector.tensor_tensor(dst4, dst4, pair(i), ALU.add))
                pairs.free(i, m)
            x_stored[b] = x_slot_free[b % 2] = load(
                "x_store", x_store[b].rearrange("(t p) d -> p t d", p=P), xb, m)
            yield 3

        def mixture(at):
            h2 = sb("h2", [P, KD, 2, B * T], F32R, at=at)
            w1 = sb("w1", [P, 2, KD, 2, FF], F32R, at=at)
            w2 = sb("w2", [P, 2, KF, 2, D], F32R, at=at)
            raw = sb("raw_e", [P, 2, BANK], at=at)
            eb1 = sb("eb1", [P, E, KF], at=at)
            mid = sb("mid", [P, KF, 2, BANK], F32R, at=at)
            gl = sb("gl", [P, 3, BANK], at=at)
            X = sb("X_all", [P, B, TT, D], at=at)
            x_ready = [load(f"x_back{b}", X[:, b], x_store[b].rearrange("(t p) d -> p t d", p=P), x_stored[b])
                       for b in range(B)]
            raws, gls, hbanks, obanks = Ring(2), Ring(3), Ring(4), Ring(2)
            act.wait(load("eb1", eb1[:], io["cols_L0_ffn_e_b1"]))

            def split(engine, ns, dst_hi, dst_lo, src, *marks):
                engine.wait(*marks)
                m = engine.done(ns.tensor_copy(dst_hi, src))
                engine.wait(m)
                return engine.done(ns.tensor_tensor(dst_lo, src, dst_hi.bitcast(F32), ALU.subtract))

            w_free = {("w1", 0): None, ("w1", 1): None, ("w2", 0): None, ("w2", 1): None}

            def expert_weights(e):
                marks = []
                W1, W2 = (io[n][e].rearrange("(k p) n -> p k n", p=P) for n in ("L0_ffn_e_w1", "L0_ffn_e_w2"))
                c1 = [(slice(k, k + 1), slice(n, n + BANK)) for k in range(KD) for n in range(0, FF, BANK)]
                c2 = [(slice(k, k + BANK // D), slice(0, D)) for k in range(0, KF, BANK // D)]
                for name, dst, src, pieces in (("w1", w1, W1, c1), ("w2", w2, W2, c2)):
                    for ks_, ns_ in pieces:
                        r, free = raws.take()
                        flat = raw[:, r, :].rearrange("p (k n) -> p k n", k=ks_.stop - ks_.start)
                        m = load(f"raw{r}", flat, src[:, ks_, ns_], *free)
                        m = split(pool, nc.gpsimd, dst[:, e % 2, ks_, 0, ns_], dst[:, e % 2, ks_, 1, ns_],
                                  flat, m, w_free[name, e % 2])
                        raws.free(r, m)
                    marks.append(m)
                return marks

            w_ready = [expert_weights(0)]
            h2_ready = []
            for b in range(B):
                for t0 in range(0, T, BANK):
                    for k in range(KD):
                        r, free = raws.take()
                        m = load(f"raw{r}", raw[:, r, :], h2_store[b, k, :, t0:t0 + BANK], h2_stored[b], *free)
                        o = slice(b * T + t0, b * T + t0 + BANK)
                        m = split(dve, nc.vector, h2[:, k, 0, o], h2[:, k, 1, o], raw[:, r, :], m)
                        raws.free(r, m)
                    h2_ready.append(m)

            mid_free = [None] * KF
            PARTS = ((0, 0), (0, 1), (1, 0))

            def up(e, c, f):
                i, free = hbanks.take()
                pe.wait(w_ready[e][0], h2_ready[c], *free)
                for k in range(KD):
                    for a, bb in PARTS:
                        m = nc.tensor.matmul(PS[:, i, :], w1[:, e % 2, k, a, f * P:(f + 1) * P],
                                             h2[:, k, bb, c * BANK:(c + 1) * BANK],
                                             start=(k == 0 and (a, bb) == (0, 0)),
                                             stop=(k == KD - 1 and (a, bb) == PARTS[-1]))
                h_m = pe.done(m)
                g, free = gls.take()
                act.wait(h_m, *free)
                m = act.done(nc.scalar.activation(gl[:, g, :], PS[:, i, :], ACT.Gelu, bias=eb1[:, e, f:f + 1]))
                hbanks.free(i, m)
                return h_m, g, m

            def down(e, c, f, o, mid_m):
                pe.wait(mid_m, w_ready[e][1])
                for t in range(BANK // P):
                    acc = PS[:, 4 + 2 * o + t // 2, (t % 2) * D:(t % 2 + 1) * D]
                    for a, bb in PARTS:
                        first = f == 0 and t % 2 == 0 and (a, bb) == (0, 0)
                        m = nc.tensor.matmul(acc, mid[:, f, a, t * P:(t + 1) * P], w2[:, e % 2, f, bb, :],
                                             start=first, stop=(f == KF - 1 and (a, bb) == PARTS[-1]),
                                             skip_group_check=True)
                return pe.done(m)

            chunks = [(e, c) for e in range(E) for c in range(CH)]
            mid_m, o_slot = {}, {}
            for n in range(len(chunks) + 1):
                for f in range(KF):
                    if n < len(chunks):
                        e, c = chunks[n]
                        h_m, g, g_m = up(e, c, f)
                    if n > 0:
                        pe_, pc = chunks[n - 1]
                        if f == 0:
                            o_slot[n - 1], free = obanks.take()
                            pe.wait(*free)
                        d_m = mid_free[f] = down(pe_, pc, f, o_slot[n - 1], mid_m[f])
                    if n < len(chunks):
                        mid_m[f] = split(dve, nc.vector, mid[:, f, 0, :], mid[:, f, 1, :], gl[:, g, :],
                                         g_m, mid_free[f])
                        gls.free(g, mid_m[f])
                if n < len(chunks) and c == CH - 1:
                    w_free["w1", e % 2] = h_m
                if n > 0:
                    e, c = chunks[n - 1]
                    b = c * BANK // T
                    dve.wait(d_m, x_ready[b])
                    for t in range(BANK // P):
                        tile = (c * BANK % T) // P + t
                        m = dve.done(nc.vector.scalar_tensor_tensor(
                            X[:, b, tile, :], PS[:, 4 + 2 * o_slot[n - 1] + t // 2, (t % 2) * D:(t % 2 + 1) * D],
                            WT[:, b, tile, e:e + 1], X[:, b, tile, :], ALU.mult, ALU.add))
                    obanks.free(o_slot[n - 1], m)
                    x_ready[b] = m
                    if e == E - 1 and (c + 1) * BANK % T == 0:
                        out_m = load("out", out[b].rearrange("(t p) d -> p t d", p=P), X[:, b], m)
                    if c == CH - 1:
                        w_free["w2", e % 2] = d_m
                if n < len(chunks) and chunks[n][1] == 1 and chunks[n][0] + 1 < E:
                    w_ready.append(expert_weights(chunks[n][0] + 1))
            sync.wait(out_m)

        def load_weights(table, room=None, *marks):
            w, at = {}, 0
            for name, (shape, parts, zero) in table.items():
                if room is None:
                    t = fb(f"w_{name}", shape)[:]
                else:
                    size = 1
                    for n in shape[1:]:
                        size *= n
                    t = room[0:shape[0], at:at + size]
                    at += size
                    if len(shape) == 3:
                        t = t.rearrange("p (k n) -> p k n", k=shape[1])
                w[name] = t
                z_m = None
                if zero:
                    pool.wait(*marks)
                    z_m = pool.done(nc.gpsimd.memset(t, 0.0))
                for dst, src in parts(t):
                    w_m = load("weights", dst, src, z_m, *marks)
            return w, w_m

        def room_for(table):
            total = 0
            for shape, _, _ in table.values():
                size = 1
                for n in shape[1:]:
                    size *= n
                total += size
            return total

        def rows(name, k):
            src = io[name]
            return ([P, k, src.shape[1]], lambda t: [(t, src.rearrange("(k p) n -> p k n", p=P))], False)

        def column(name, k):
            return ([P, k], lambda t: [(t, io["cols_" + name])], False)

        def row(name):
            return ([1, io[name].shape[0]], lambda t: [(t, io[name].unsqueeze(0))], False)

        def head_rows(name):
            src = io[name]
            return ([P, G, D], lambda t: [(t[32 * j:32 * j + HD, :, :],
                                           src.rearrange("(g j d) n -> j d g n", j=HG, d=HD)[j])
                                          for j in range(HG)], True)

        h2_stored, x_stored = [None] * B, [None] * B
        mamba_table = {
            "norm": column("L0_attn_norm_w", KD), "in": rows("L0_attn_in_proj_w", KD),
            "bc": ([P, KI, 2 * N], lambda t: [
                (t[:, :, 0:N], io["L0_attn_B_proj_w"].rearrange("(k p) n -> p k n", p=P)),
                (t[:, :, N:2 * N], io["L0_attn_C_proj_w"].rearrange("(k p) n -> p k n", p=P))], False),
            "A": rows("L0_attn_A_proj_w", KI), "Ab_half": column("L0_attn_A_proj_b", KI),
            "Dw": column("L0_attn_D", KI), "out": rows("L0_attn_out_proj_w", KI),
            "abase_half": ([P, N], lambda t: [(t, io["L0_attn_A_base"].partition_broadcast(P))], False),
        }
        cross_table = {
            "xWq": rows("L0_xattn_Wq", KD), "xbq": column("L0_xattn_bq", KD),
            "xWk": rows("L0_xattn_Wk", KD), "xbk": column("L0_xattn_bk", KD),
            "xWv": rows("L0_xattn_Wv", KD), "xbv": row("L0_xattn_bv"),
            "xWo": head_rows("L0_xattn_Wo"), "xbo": row("L0_xattn_bo"),
        }
        self_table = {
            "g1": column("L0_ffn_ln1_g", KD), "b1": column("L0_ffn_ln1_b", KD),
            "g2": column("L0_ffn_ln2_g", KD), "b2": column("L0_ffn_ln2_b", KD),
            "Wq": rows("L0_ffn_Wq", KD), "bq": column("L0_ffn_bq", KD),
            "Wk": rows("L0_ffn_Wk", KD), "bk": column("L0_ffn_bk", KD),
            "Wv": rows("L0_ffn_Wv", KD), "bv": row("L0_ffn_bv"),
            "Wo": head_rows("L0_ffn_Wo"), "bo": row("L0_ffn_bo"),
            "Wr": rows("L0_ffn_Wr", KD), "br": row("L0_ffn_br"),
            "eb2": ([E, D], lambda t: [(t, io["L0_ffn_e_b2"])], False),
        }
        w_scan, w_m = load_weights(mamba_table)
        pe.wait(w_m)
        act.wait(w_m)
        m = act.done(nc.scalar.activation(w_scan["abase_half"], w_scan["abase_half"], ACT.Tanh, scale=0.5))
        dve.wait(m, w_m)
        m = dve.done(nc.vector.tensor_scalar(w_scan["abase_half"], w_scan["abase_half"], 0.25, 0.25,
                                             ALU.mult, ALU.add))
        m = dve.done(nc.vector.tensor_scalar(w_scan["Ab_half"], w_scan["Ab_half"], 0.5, None, ALU.mult))
        act.wait(m)
        w_room = fb("w_room", [P, max(room_for(cross_table), room_for(self_table))])
        scans, attns = Stream(), Stream()

        def attention_blocks(b):
            if stages >= 2:
                yield from cross_block(b)
            if stages >= 3:
                yield from self_block(b)
            else:
                x_stored[b] = x_slot_free[b % 2] = load(
                    "x_store", x_store[b].rearrange("(t p) d -> p t d", p=P), X[:, b % 2], *attns.last.values(), x_ready[b])

        SCAN_LENGTH, ATTN_LENGTH = 400.0, 700.0
        for b in range(B + 1):
            tracks = []
            if b > 0:
                tracks.append((attns, attention_blocks(b - 1), ATTN_LENGTH))
            if b < B:
                tracks.append((scans, scan_block(b, w_scan), SCAN_LENGTH))
            total = [0.0] * len(tracks)
            for _ in weave(*tracks):
                pass
        for ln in (pe, act, dve, pool, sync):
            ln.wait(*scans.last.values(), *attns.last.values())
        fr.close()
        if stages >= 4:
            with ExitStack() as at:
                mixture(at)
        else:
            for b in range(B):
                m = load("out", out[b], x_store[b], x_stored[b])
            sync.wait(m)


_COLUMNS = ["L0_attn_norm_w", "L0_attn_A_proj_b", "L0_attn_D", "L0_xattn_bq", "L0_xattn_bk",
            "L0_ffn_ln1_g", "L0_ffn_ln1_b", "L0_ffn_ln2_g", "L0_ffn_ln2_b", "L0_ffn_bq", "L0_ffn_bk"]
_OUT_SHAPE = (4, 1024, 256)


def kernel(**inputs):
    import numpy as np
    import concourse.bacc as bacc
    from concourse.bass_utils import run_bass_kernel_spmd as run

    nc = bacc.Bacc("TRN2", target_bir_lowering=False, num_devices=1)
    r = np.arange(128)
    consts = {
        "c_ident": np.eye(128, dtype=np.float32),
        "c_masks": np.stack([np.where(r[None, :] > r[:, None], MASKED, 0.0),
                             np.where(r[:, None] > r[None, :], MASKED, 0.0)], 1).astype(np.float32),
        "c_sel": (r[:, None] == 32 * np.arange(4)[None, :] + 16).astype(np.float32),
        "c_ones": np.ones((1, 128), np.float32),
    }
    columns = {"cols_" + name: np.asarray(inputs[name]).reshape(-1, 128).T for name in _COLUMNS}
    eb1 = np.asarray(inputs["L0_ffn_e_b1"])
    columns["cols_L0_ffn_e_b1"] = eb1.reshape(eb1.shape[0], -1, 128).transpose(2, 0, 1)
    arrays, io = {}, {}
    for name, value in {**inputs, **columns, **consts}.items():
        a = np.ascontiguousarray(value)
        arrays["in_" + name] = a
        io[name] = nc.dram_tensor("in_" + name, a.shape, mybir.dt.from_np(a.dtype), kind="ExternalInput").ap()
    out = nc.dram_tensor("out_x", _OUT_SHAPE, F32, kind="ExternalOutput").ap()
    decoder_layer(nc, io, out, STAGES)
    result = run(nc, [arrays], core_ids=[0])
    return result.results[0]["out_x"]
```

```python
from contextlib import ExitStack

import concourse.bass as bass
from concourse import mybir

F32 = mybir.dt.float32
F32R = mybir.dt.float32r
BF16 = mybir.dt.bfloat16
ALU = mybir.AluOpType
ACT = mybir.ActivationFunctionType
AX = mybir.AxisListType

P = 128
BANK = 512
MASKED = -1.0e30
STAGES = 4


class Stream:

    current = None

    def __init__(self):
        self.last = {}

    @staticmethod
    def note(mark):
        if Stream.current is not None:
            Stream.current.last[id(mark[0])] = mark
        return mark


def weave(*tracks):
    at = [0.0] * len(tracks)
    live = set(range(len(tracks)))
    outer = Stream.current
    while live:
        n = min(live, key=lambda k: at[k] / tracks[k][2])
        if tracks[n][0] is not None:
            Stream.current = tracks[n][0]
        step = next(tracks[n][1], None)
        if step is None:
            live.discard(n)
        else:
            at[n] += step
        Stream.current = outer
        if step is not None:
            yield step


class Line:

    def __init__(self, eng, sem):
        self.eng, self.sem, self.count, self.seen = eng, sem, 0, {}

    def done(self, instruction):
        instruction.then_inc(self.sem, 1)
        self.count += 1
        return Stream.note((self.sem, self.count))

    def wait(self, *marks):
        for mark in marks:
            if mark is not None and self.seen.get(id(mark[0]), 0) < mark[1]:
                self.eng.wait_ge(mark[0], mark[1])
                self.seen[id(mark[0])] = mark[1]


class Lane:

    def __init__(self, sem):
        self.sem, self.count = sem, 0

    def done(self, instruction):
        instruction.then_inc(self.sem, 16)
        self.count += 16
        return Stream.note((self.sem, self.count))


class Ring:

    def __init__(self, n):
        self.idle = [(i, []) for i in range(n)]

    def take(self):
        assert self.idle, "no buffer whose readers are all queued"
        return self.idle.pop(0)

    def free(self, i, *marks):
        self.idle.append((i, list(marks)))


def decoder_layer(nc, io, out, stages=4):
    x, ctxt = io["x"], io["ctx_1024"]
    B, T, D = x.shape
    S = ctxt.shape[1]
    DIN = io["L0_attn_A_proj_w"].shape[0]
    N = io["L0_attn_A_base"].shape[0]
    E, _, FF = io["L0_ffn_e_w1"].shape
    H = 16
    HD = D // H
    KD, KI, KF = D // P, DIN // P, FF // P
    TT = T // P
    NH2 = T // BANK
    SB = S // 2
    HG = 4
    G = H // HG
    SCALE = float(HD) ** -0.5

    scan_bc = nc.dram_tensor("scan_bc", (B, 2 * N, T), F32, kind="Internal").ap()
    stores = {name: [nc.dram_tensor(f"{name}_store{b}", (D // (HG * HD), 3, HD, HG, n), BF16, kind="Internal").ap()
                     for b in range(B)] for name, n in (("xq", T), ("xk", S), ("q", T), ("k", T))}

    ctx = ExitStack()
    with ctx:
        def sem(name):
            return ctx.enter_context(nc.semaphore(name))

        def sb(name, shape, dt=F32, at=ctx, side=None):
            return at.enter_context(nc.sbuf_tensor(name, shape, dt, side=side))

        pe, act = Line(nc.tensor, sem("pe_done")), Line(nc.scalar, sem("act_done"))
        dve, pool = Line(nc.vector, sem("dve_done")), Line(nc.gpsimd, sem("pool_done"))
        sync = Line(nc.sync, sem("sync_unused"))
        lanes = {}

        def lane(name):
            if name not in lanes:
                lanes[name] = Lane(sem("dma_" + name))
            return lanes[name]

        def load(name, dst, src, *marks):
            sync.wait(*marks)
            return lane(name).done(nc.sync.dma_start(dst, src))

        PS = ctx.enter_context(nc.psum_tensor("PS", [P, 8, BANK], F32))
        pairs = Ring(3)

        def pair(i):
            return PS[:, 2 * i:2 * i + 2, :].rearrange("p a b -> p (a b)")

        WT = sb("WT", [P, B, TT, E])
        ident = sb("ident", [P, P])
        ident_bf = sb("ident_bf", [P, P], BF16)
        masks = sb("masks", [P, 2, P])
        masks_bf = sb("masks_bf", [P, 2, P], BF16)
        ones_row = sb("ones_row", [1, P])
        sel_sum = sb("sel_sum", [P, HG])
        half = sb("half", [P, TT])

        load("const", ident[:], io["c_ident"])
        load("const", masks[:], io["c_masks"])
        load("const", sel_sum[:], io["c_sel"])
        const_in = load("const", ones_row[:], io["c_ones"])
        dve.wait(const_in)
        dve.done(nc.vector.tensor_copy(ident_bf[:], ident[:]))
        const_ready = dve.done(nc.vector.tensor_copy(masks_bf[:], masks[:]))
        gather_clear = dve.done(nc.vector.memset(PS[:, 6:8, :], 0.0))
        half_ready = pool.done(nc.gpsimd.memset(half[:], -0.5))
        pe.wait(const_in, const_ready, gather_clear)

        def settle(*more):
            for ln in (pe, act, dve, pool, sync):
                ln.wait(*Stream.current.last.values(), *more)

        def mean_var(stats, moments, src, *marks):
            dve.wait(*marks)
            for t in range(TT):
                m = dve.done(nc.vector.bn_stats(stats[:, t, :], src(t)))
            dve.wait(m)
            for t in range(TT):
                m = dve.done(nc.vector.bn_aggr(moments[:, t, :], stats[:, t, :]))
            return m

        def rsqrt(dst, tmp, src, eps, *marks):
            dve.wait(*marks)
            m = dve.done(nc.vector.tensor_scalar(tmp, src, eps, None, ALU.add))
            pool.wait(m, half_ready)
            return pool.done(nc.gpsimd.tensor_tensor(dst, tmp, half[:, 0:TT], ALU.pow))

        def norm_scales(sc, moments, eps, inner_eps, m):
            var = moments[:, :, 1]
            m1 = rsqrt(sc[:, 0, :], sc[:, 2, :], var, eps, m)
            yield 2
            if inner_eps is None:
                return m1, sc[:, 0, :]
            dve.wait(m1)
            m = dve.done(nc.vector.tensor_tensor(sc[:, 3, :], sc[:, 0, :], sc[:, 0, :], ALU.mult))
            dve.wait(m)
            m = dve.done(nc.vector.tensor_tensor(sc[:, 3, :], sc[:, 3, :], var, ALU.mult))
            m = rsqrt(sc[:, 1, :], sc[:, 2, :], sc[:, 3, :], inner_eps, m)
            yield 2
            dve.wait(m)
            m = dve.done(nc.vector.tensor_tensor(sc[:, 1, :], sc[:, 0, :], sc[:, 1, :], ALU.mult))
            return m, sc[:, 1, :]

        def normed(dst, b_t, moments, t, scale):
            return dve.done(nc.vector.tensor_scalar(dst, b_t, moments[:, t, 0:1], scale[:, t:t + 1],
                                                    ALU.subtract, ALU.mult))

        def transpose_tokens(dst, src, scale, bias, *marks):
            for k in range(KD):
                i, free = pairs.take()
                pe.wait(*free, *marks)
                for t in range(TT):
                    m = nc.tensor.transpose(pair(i)[:, t * P:(t + 1) * P],
                                            src[:, t, k * P:(k + 1) * P], ident[:])
                m = pe.done(m)
                dve.wait(m)
                if scale is None:
                    m = dve.done(nc.vector.tensor_copy(dst[:, k, :], pair(i)))
                else:
                    m = dve.done(nc.vector.tensor_scalar(dst[:, k, :], pair(i), scale[:, k:k + 1],
                                                         bias[:, k:k + 1], ALU.mult, ALU.add))
                pairs.free(i, m)
            return m

        def project(dst_pair, lhs, rhs, K, width):
            for c0 in range(0, width, BANK):
                c1 = min(c0 + BANK, width)
                for k in range(K):
                    m = nc.tensor.matmul(dst_pair[:, c0:c1], lhs(k), rhs(k, c0, c1),
                                         start=(k == 0), stop=(k == K - 1))
            return m

        TQ = T // 4
        QTT = TQ // P
        X = sb("X", [P, 2, TT, D])
        m_st, m_mv, m_sc = sb("m_st", [P, TT, 6]), sb("m_mv", [P, TT, 2]), sb("m_sc", [P, 4, TT])
        m_xs, m_xT = sb("m_xs", [P, QTT, D]), sb("m_xT", [P, 2, KD, TQ])
        xh = sb("xh", [P, D])
        xin2, th2 = sb("xin", [P, 2, KI, TQ]), sb("th", [P, 2, KI, TQ])
        z, y = sb("z", [P, KI, TQ]), sb("y", [P, KI, TQ])
        bcs = sb("bcs", [2 * N, TQ])
        bc = sb("bc", [P, 3, 2, TQ])
        decay = sb("decay", [P, 2, KI, TQ])
        drive = sb("drive", [P, 3, KI, TQ])
        state = sb("state", [P, N, KI])
        bc_ring, rd, rv = Ring(3), Ring(2), Ring(3)
        DVE_ADDS = (2, 99)
        x_ready = [None] * B
        x_slot_free = [None, None]

        def flat(t):
            return t.rearrange("p a b -> p (a b)")

        def scan_block(b, w):
            xb = X[:, b % 2]
            settle()
            x_ready[b] = load(f"x{b % 2}", xb, x[b].rearrange("(t p) d -> p t d", p=P), x_slot_free[b % 2])
            m = mean_var(m_st, m_mv, lambda t: xb[:, t, :], x_ready[b])
            sc_m, r12 = yield from norm_scales(m_sc, m_mv, 1e-5, 1e-6, m)
            yield 3

            NQ = T // TQ
            ready = {}
            ended = {}

            def prepare(q):
                s2 = q % 2
                xin, th, xT_q = xin2[:, s2], th2[:, s2], m_xT[:, s2]
                dve.wait(sc_m, ready.get(q - 1, {}).get("turned"))
                for t in range(QTT):
                    m = normed(m_xs[:, t, :], xb[:, q * QTT + t, :], m_mv, q * QTT + t, r12)
                i, free = pairs.take()
                pe.wait(*free, m)
                for k in range(KD):
                    for t in range(QTT):
                        m = nc.tensor.transpose(pair(i)[:, k * BANK + t * P:k * BANK + (t + 1) * P],
                                                m_xs[:, t, k * P:(k + 1) * P], ident[:])
                turned = m = pe.done(m)
                for t in range(q * QTT, (q + 1) * QTT):
                    x_m = normed(xh[:], xb[:, t, :], m_mv, t, m_sc[:, 0, :])
                    dve.wait(x_m)
                    x_m = dve.done(nc.vector.tensor_tensor(xb[:, t, :], xb[:, t, :], xh[:], ALU.add))
                    dve.wait(x_m)
                act.wait(m, *ended.get(q - 2, []))
                for k in range(KD):
                    m = act.done(nc.scalar.activation(xT_q[:, k, :], pair(i)[:, k * BANK:k * BANK + TQ],
                                                      ACT.Identity, scale=w["norm"][:, k:k + 1]))
                pairs.free(i, m)
                xT_m = m
                yield 3
                pe.wait(m)
                i, free = pairs.take()
                pe.wait(*free)
                for c in range(KI):
                    m = project(pair(i)[:, c * TQ:(c + 1) * TQ],
                                lambda k: w["in"][:, k, c * P:(c + 1) * P],
                                lambda k, c0, c1: xT_q[:, k, c0:c1], KD, TQ)
                m = pe.done(m)
                act.wait(m)
                m = xin_m = act.done(nc.scalar.activation(flat(xin), pair(i), ACT.Silu))
                pairs.free(i, m)
                yield 4
                pe.wait(m)
                i, free = pairs.take()
                pe.wait(*free)
                m = pe.done(project(pair(i)[0:2 * N, 0:TQ], lambda k: w["bc"][:, k, :],
                                    lambda k, c0, c1: xin[:, k, c0:c1], KI, TQ))
                act.wait(m, ready.get(q - 1, {}).get("stored"))
                m = act.done(nc.scalar.copy(bcs[:], pair(i)[0:2 * N, 0:TQ]))
                pairs.free(i, m)
                stored = load("bc_store", scan_bc[b, :, q * TQ:(q + 1) * TQ], bcs[:], m)
                yield 2
                i, free = pairs.take()
                pe.wait(*free)
                for c in range(KI):
                    m = project(pair(i)[:, c * TQ:(c + 1) * TQ], lambda k: w["A"][:, k, c * P:(c + 1) * P],
                                lambda k, c0, c1: xin[:, k, c0:c1], KI, TQ)
                m = pe.done(m)
                act.wait(m)
                for c in range(KI):
                    m = act.done(nc.scalar.activation(th[:, c, :], pair(i)[:, c * TQ:(c + 1) * TQ],
                                                      ACT.Tanh, bias=w["Ab_half"][:, c:c + 1], scale=0.5))
                pairs.free(i, m)
                ready[q] = dict(xin=xin_m, x=x_m, xT=xT_m, stored=stored, th=m, turned=turned)
                yield 5

            def scan(q):
                s2, now, before = q % 2, ready[q], ended.get(q - 1, [])
                xin, th, xT_q = xin2[:, s2], th2[:, s2], m_xT[:, s2]
                cols = slice(q * TQ, (q + 1) * TQ)
                act.wait(now["xin"], *before)
                for c in range(KI):
                    y_mark = act.done(nc.scalar.activation(y[:, c, :], xin[:, c, :], ACT.Identity,
                                                           scale=w["Dw"][:, c:c + 1]))
                act.wait(now["th"])
                pool.wait(now["xin"])
                made, held = {}, {}

                def inputs_of(n):
                    s, free = bc_ring.take()
                    spread = load(f"bc{s}", bc[:, s, :, :],
                                  scan_bc[b, n:n + N + 1:N, cols].partition_broadcast(P),
                                  now["stored"], *free)
                    i, free = rd.take()
                    act.wait(*free)
                    d_m = act.done(nc.scalar.activation(flat(decay[:, i]), flat(th), ACT.Identity,
                                                        bias=w["abase_half"][:, n:n + 1],
                                                        scale=w["abase_half"][:, n:n + 1]))
                    j, free = rv.take()
                    pool.wait(spread, *free)
                    v_m = pool.done(nc.gpsimd.tensor_tensor(
                        drive[:, j], xin, bc[:, s, 0:1, :].to_broadcast([P, KI, TQ]), ALU.mult))
                    made[n] = s, spread, i, d_m, j, v_m

                def add_to_y(n):
                    nonlocal y_mark
                    g, c_m = held.pop(n)
                    adder, ns = (dve, nc.vector) if n % DVE_ADDS[b > 0] == 1 else (pool, nc.gpsimd)
                    adder.wait(c_m, y_mark)
                    y_mark = adder.done(ns.tensor_tensor(flat(y[:]), flat(y[:]), flat(drive[:, g]), ALU.add))
                    rv.free(g, y_mark)

                inputs_of(0)
                for n in range(N):
                    if n + 1 < N:
                        inputs_of(n + 1)
                    s, spread, i, d_m, j, v_m = made.pop(n)
                    dve.wait(d_m, v_m)
                    for c in range(KI):
                        h_m = dve.done(nc.vector.tensor_tensor_scan(
                            drive[:, j, c, :], decay[:, i, c, :], drive[:, j, c, :],
                            0.0 if q == 0 else state[:, n, c:c + 1], ALU.mult, ALU.add))
                    rd.free(i, h_m)
                    dve.wait(h_m, spread)
                    s_m = dve.done(nc.vector.tensor_copy(state[:, n, :], drive[:, j, :, TQ - 1]))
                    dve.wait(s_m)
                    c_m = dve.done(nc.vector.tensor_tensor(
                        drive[:, j], drive[:, j], bc[:, s, 1:2, :].to_broadcast([P, KI, TQ]), ALU.mult))
                    held[n] = j, c_m
                    bc_ring.free(s, c_m, v_m)
                    if n > 0:
                        add_to_y(n - 1)
                    if n == N // 2:
                        i, free = pairs.take()
                        pe.wait(now["xT"], *free)
                        for c in range(KI):
                            m = project(pair(i)[:, c * TQ:(c + 1) * TQ],
                                        lambda k: w["in"][:, k, DIN + c * P:DIN + (c + 1) * P],
                                        lambda k, c0, c1: xT_q[:, k, c0:c1], KD, TQ)
                        m = pe.done(m)
                        act.wait(m, *before)
                        z_ready = act.done(nc.scalar.activation(flat(z[:]), pair(i), ACT.Silu))
                        pairs.free(i, z_ready)
                    yield 5
                dve.wait(s_m)
                add_to_y(N - 1)
                yield 2
                dve.wait(y_mark, z_ready)
                m = dve.done(nc.vector.tensor_tensor(flat(y[:]), flat(y[:]), flat(z[:]), ALU.mult))
                i, free = pairs.take()
                pe.wait(*free, m)
                for t in range(QTT):
                    for k in range(KI):
                        m = nc.tensor.matmul(pair(i)[:, t * D:(t + 1) * D], y[:, k, t * P:(t + 1) * P],
                                             w["out"][:, k, :], start=(k == 0), stop=(k == KI - 1))
                m = pe.done(m)
                ended[q] = [m, y_mark, c_m]
                dst = flat(xb[:, q * QTT:(q + 1) * QTT, :])
                dve.wait(m, now["x"])
                m = dve.done(nc.vector.tensor_tensor(dst, dst, pair(i)[:, 0:QTT * D], ALU.add))
                x_ready[b] = m
                pairs.free(i, m)
                yield 3

            yield from prepare(0)
            for q in range(NQ):
                tracks = [(None, scan(q), 88.0)]
                if q + 1 < NQ:
                    tracks.append((None, prepare(q + 1), 14.0))
                yield from weave(*tracks)

        eb1 = sb("eb1", [P, E, KF])
        h2s, h2_ready = [None] * B, [None] * B

        def attention_phase(b, at, far):
            settle()

            def ab(name, shape, dt=F32):
                return sb(f"{name}_{b}", shape, dt, at=at)

            w_room = ab("w_room", [P, max(room_for(cross_table), room_for(self_table))])
            STACK = (((0, 1, 2), 0), ((0, 1), 1), ((0,), 2))
            ROWS = 6 * HD
            QW = BANK
            QT = QW // P
            A = ab("A", [P, TT, D])
            xT = ab("xT", [P, KD, T])
            shared = ab("tokens_or_parts", [P, 3, T])
            xs = shared[:, 0:2, :].rearrange("p a (t d) -> p (a t) d", d=D)
            st, mv, sc = ab("st", [P, TT, 6]), ab("mv", [P, TT, 2]), ab("sc", [P, 4, TT])
            va = ab("va", [P, TT, H, HD + 1])
            parts = flat(shared[:]).bitcast(BF16).rearrange("p (s r n) -> p s r n", s=2, r=3)
            rest = ab("rest", [P, T])
            qs = ab("qs", [P, 3, HG, QW], BF16)
            ks = ab("ks", [P, 2, HG, T], BF16)
            mx, mx_rest = ab("mx", [P, 2, QT, HG]), ab("mx_rest", [P, QT, HG])
            neg = ab("neg", [P, 2, QT, HG, 3], BF16)
            pt = sb(f"pt_{b}", [P, 4, 2, QW], at=far, side="right")
            raw = ab("raw", [P, 2, QW])
            rq = ab("rq", [P, QT, HG])
            oT = ab("oT", [P, 2, QW])
            qslots, kslots, ptr, partr, restr = Ring(3), Ring(2), Ring(4), Ring(2), Ring(1)
            mxr, negr, rawr, gath, oTr = Ring(2), Ring(2), Ring(2), Ring(2), Ring(2)
            ones_ready = None
            dve.done(nc.vector.memset(qs[ROWS:P], 0.0))
            ones_ready = dve.done(nc.vector.memset(ks[ROWS:P], 1.0))
            va_ready = pool.done(nc.gpsimd.memset(va[:], 1.0))

            def split_projection(name, store, srcT, weight, bias, width, ready):
                pe.wait(ready)
                for c in range(KD):
                    i, free = pairs.take()
                    pe.wait(*free)
                    m = pe.done(project(pair(i), lambda k: weight[:, k, c * P:(c + 1) * P],
                                        lambda k, c0, c1: srcT[:, k, c0:c1], KD, width))
                    s, free = partr.take()
                    act.wait(m, *free)
                    p0, p1, p2 = (parts[:, s, r, 0:width] for r in range(3))
                    m = act.done(nc.scalar.activation(p0, pair(i)[:, 0:width], ACT.Identity,
                                                      bias=bias[:, c:c + 1]))
                    _, free = restr.take()
                    dve.wait(m, *free)
                    r_m = dve.done(nc.vector.scalar_tensor_tensor(
                        rest[:, 0:width], pair(i)[:, 0:width], bias[:, c:c + 1], p0, ALU.add, ALU.subtract))
                    pairs.free(i, r_m)
                    act.wait(r_m)
                    m = act.done(nc.scalar.copy(p1, rest[:, 0:width]))
                    dve.wait(m)
                    split = dve.done(nc.vector.tensor_tensor(p2, rest[:, 0:width], p1, ALU.subtract))
                    restr.free(0, split)
                    rows_of = HG * HD
                    for g in range(P // rows_of):
                        for r in range(3):
                            m = load(f"{name}_parts{s}", store[c * (P // rows_of) + g, r].rearrange("d j n -> j d n"),
                                     parts[g * rows_of:(g + 1) * rows_of, s, r, 0:width], split)
                    partr.free(s, m)
                    yield m

            def attention(q_store, k_store, kwidth, blocks, causal, stored, weight, bias_row, dst, dst_m):

                def stack(lane_name, to, source, *marks):
                    row = 0
                    sync.wait(*marks)
                    for term in STACK:
                        n = len(term[0])
                        m = load(lane_name, to[row:row + n * HD], source(term))
                        row += n * HD
                    return m

                def fetch_keys(g):
                    s, free = kslots.take()
                    return s, stack(f"ks{s}", ks[:, s, :, 0:kwidth],
                                    lambda term: k_store[g, term[1]:term[1] + 1].rearrange("r d j n -> r d (j n)")
                                    .to_broadcast([len(term[0]), HD, HG * kwidth]), *stored, *free)

                def fetch_queries(g, q0):
                    u, free = qslots.take()
                    z_m = load(f"qs{u}", flat(qs[ROWS:ROWS + 3, u]).bitcast(F32), io["c_zeros"],
                               ones_ready, *free)
                    return u, z_m, stack(f"qs{u}", qs[:, u],
                                    lambda term: q_store[g, 0:len(term[0]), :, :, q0:q0 + QW]
                                    .rearrange("r d j n -> (r d) j n"), *stored, *free)

                def head(t, slot, j, rows):
                    return t[0:rows, slot, j, :]

                def first_pass(g, q0, kslot, k_m, u, z_m, q_m, result):
                    x_, free_mx = mxr.take()
                    pe.wait(q_m, k_m, z_m, ones_ready)
                    dve.wait(*free_mx)

                    def reduce(i, m, t, j0, per, keys):
                        dve.wait(m)
                        src = pair(i)
                        if per == 4:
                            src = src.rearrange("p (b a k) -> p a b k", b=2, a=2)[:, :, :, 0:keys]
                        elif per == 2:
                            src = src.rearrange("p (j k) -> p j k", j=2)[:, :, 0:keys]
                        else:
                            src = src[:, 0:keys]
                        m = dve.done(nc.vector.tensor_reduce(mx[:, x_, t, j0:j0 + per], src, AX.X, ALU.max))
                        pairs.free(i, m)
                        return m

                    behind = None
                    for t in range(QT):
                        keys = q0 + (t + 1) * P if causal else kwidth
                        per = 4 if keys <= BANK // 2 else 2 if keys <= BANK else 1
                        for j0 in range(0, HG, per):
                            i, free = pairs.take()
                            pe.wait(*free)
                            for j in range(j0, j0 + per):
                                base = (0 if per == 1 else (j % 2) * BANK + (j - j0) // 2 * (BANK // 2))
                                for c0 in range(0, keys, BANK):
                                    c1 = min(c0 + BANK, keys)
                                    diag = causal and c1 == keys
                                    m = nc.tensor.matmul(pair(i)[:, base + c0:base + c1],
                                                         head(qs, u, j, P)[:, t * P:(t + 1) * P],
                                                         head(ks, kslot, j, P)[:, c0:c1],
                                                         start=True, stop=not diag)
                                    if diag:
                                        m = nc.tensor.matmul(pair(i)[:, base + keys - P:base + keys], ident_bf[:],
                                                             masks_bf[:, 0, :], start=False, stop=True)
                            m = pe.done(m)
                            if behind is not None:
                                reduce(*behind)
                            behind = i, m, t, j0, per, keys
                            yield per * keys / 500
                    m = reduce(*behind)
                    v, free = negr.take()
                    dve.wait(m, *free)
                    m = dve.done(nc.vector.tensor_scalar(neg[:, v, :, :, 0], mx[:, x_], -1.0, None, ALU.mult))
                    dve.wait(m)
                    m = dve.done(nc.vector.scalar_tensor_tensor(mx_rest[:], mx[:, x_], -1.0, neg[:, v, :, :, 0],
                                                                ALU.mult, ALU.subtract))
                    dve.wait(m)
                    mxr.free(x_, m)
                    m = dve.done(nc.vector.tensor_copy(neg[:, v, :, :, 1], mx_rest[:]))
                    dve.wait(m)
                    m = dve.done(nc.vector.tensor_tensor(neg[:, v, :, :, 2], mx_rest[:], neg[:, v, :, :, 1],
                                                         ALU.subtract))
                    yield 1
                    for j0 in range(0, HG, 2):
                        i, free = pairs.take()
                        pe.wait(m, *free)
                        for j in (j0, j0 + 1):
                            for t in range(QT):
                                c0 = (j - j0) * BANK + t * P
                                p_m = nc.tensor.matmul(pair(i)[ROWS:ROWS + 3, c0:c0 + P], neg[:, v, t, j, :],
                                                       ident_bf[:], start=True, stop=True)
                        p_m = pe.done(p_m)
                        act.wait(p_m)
                        q_m = act.done(nc.scalar.copy(qs[ROWS:ROWS + 3, u, j0:j0 + 2, :],
                                                      pair(i)[ROWS:ROWS + 3].rearrange("p (j k) -> p j k", j=2)))
                        pairs.free(i, q_m)
                    negr.free(v, p_m)
                    result.append((u, q_m))
                    yield 1

                def second_pass(g, q0, kslot, u, q_m, result):
                    o, free = gath.take()
                    gather = PS[:, 6 + o, :]
                    pe.wait(ones_ready, q_m, *free)
                    used = [n for n, (k0, _) in enumerate(blocks) if not causal or k0 < q0 + QW]

                    def gather_values(n, a, ready_pt):
                        ksz = blocks[n][1]
                        pe.wait(*[m for _, m in ready_pt])
                        for j in range(HG):
                            m = nc.tensor.matmul(gather[32 * j:32 * j + HD + 1, a:QW], va[0:ksz, n, g * HG + j, :],
                                                 pt[0:ksz, ready_pt[j // 2][0], j % 2, a:QW],
                                                 start=(n == 0), stop=(n == used[-1]))
                        m = pe.done(m)
                        for k, _ in ready_pt:
                            ptr.free(k, m)
                        return m

                    behind = None
                    for n in used:
                        k0, ksz = blocks[n]
                        a = max(k0 - q0, 0) if causal else 0
                        diag = causal and k0 >= q0
                        ready_pt = []
                        for j0 in range(0, HG, 2):
                            i, free = pairs.take()
                            pe.wait(*free)
                            for j in (j0, j0 + 1):
                                base = (j - j0) * BANK
                                m = nc.tensor.matmul(pair(i)[0:ksz, base + a:base + QW],
                                                     head(ks, kslot, j, P)[:, k0:k0 + ksz],
                                                     head(qs, u, j, P)[:, a:QW], start=True, stop=not diag)
                                if diag:
                                    m = nc.tensor.matmul(pair(i)[0:ksz, base + a:base + a + P], ident_bf[:],
                                                         masks_bf[:, 1, :], start=False, stop=True)
                            m = pe.done(m)
                            k, free = ptr.take()
                            act.wait(m, *free)
                            m = act.done(nc.scalar.activation(
                                pt[0:ksz, k, :, a:QW],
                                pair(i).rearrange("p (j k) -> p j k", j=2)[0:ksz, :, a:QW], ACT.Exp, scale=SCALE))
                            pairs.free(i, m)
                            ready_pt.append((k, m))
                        if behind is not None:
                            gather_values(*behind)
                        behind = (n, a, ready_pt)
                        yield 4 * (QW - a) / 500
                    m = gather_values(*behind)
                    qslots.free(u, m)
                    result.append((g, q0, o, m))

                def finish(g, q0, o, m):
                    bank = PS[:, 6 + o, :]
                    v, free = rawr.take()
                    act.wait(m, *free)
                    r_m = act.done(nc.scalar.copy(raw[:, v, :], bank))
                    yield 1
                    pe.wait(r_m)
                    for t in range(QT):
                        m = nc.tensor.matmul(bank[:, t * HG:(t + 1) * HG], raw[:, v, t * P:(t + 1) * P],
                                             sel_sum[:], start=True, stop=True)
                    m = pe.done(m)
                    yield 1
                    dve.wait(m)
                    m = dve.done(nc.vector.reciprocal(rq[:].rearrange("p t j -> p (t j)"), bank[:, 0:QT * HG]))
                    yield 1
                    pe.wait(m)
                    for t in range(QT):
                        for j in range(HG):
                            m = nc.tensor.matmul(bank[32 * j:32 * (j + 1), t * P:(t + 1) * P],
                                                 rq[:, t, j:j + 1].to_broadcast([P, 32]), ident[:],
                                                 start=True, stop=True)
                    m = pe.done(m)
                    yield 1
                    e, free = oTr.take()
                    dve.wait(m, *free)
                    m = dve.done(nc.vector.tensor_tensor(oT[:, e, :], raw[:, v, :], bank, ALU.mult))
                    rawr.free(v, m)
                    yield 1
                    for t0 in range(0, QT, BANK // D):
                        pe.wait(m)
                        for t in range(t0, t0 + BANK // D):
                            p_o = bank[:, (t - t0) * D:(t - t0 + 1) * D]
                            m = nc.tensor.matmul(p_o, oT[:, e, t * P:(t + 1) * P], weight[:, g, :],
                                                 start=True, stop=g > 0)
                            if g == 0:
                                m = nc.tensor.matmul(p_o, ones_row[:], bias_row, start=False, stop=True)
                        p_m = pe.done(m)
                        yield 1
                        first = q0 // P + t0
                        part = flat(dst[:, first:first + BANK // D, :])
                        dve.wait(p_m, dst_m[first // (BANK // D)])
                        m = dve.done(nc.vector.tensor_tensor(part, part, bank, ALU.add))
                        dst_m[first // (BANK // D)] = m
                    oTr.free(e, p_m)
                    gath.free(o, m)
                    yield 1

                units = [(g, q0) for g in range(G) for q0 in range(0, T, QW)]
                fetched, keys_of, got = {}, {}, {}

                def fetch(n):
                    if n < len(units):
                        g, q0 = units[n]
                        if q0 == 0:
                            keys_of[g] = fetch_keys(g)
                        fetched[n] = fetch_queries(g, q0)

                def start(n, result):
                    g, q0 = units[n]
                    return first_pass(g, q0, *keys_of[g], *fetched.pop(n), result)

                fetch(0)
                fetch(1)
                first = []
                yield from start(0, first)
                gathered = None
                for n in range(len(units) + 1):
                    fetch(n + 2)
                    nxt, done, tracks = [], [], []
                    if n < len(units):
                        g, q0 = units[n]
                        tracks.append((None, second_pass(g, q0, keys_of[g][0], *first[0], done), 1.0))
                    if n + 1 < len(units):
                        tracks.append((None, start(n + 1, nxt), 1.0))
                    if gathered is not None:
                        tracks.append((None, finish(*gathered), 1.0))
                    yield from weave(*tracks)
                    if n < len(units):
                        gathered = done[0]
                        if q0 == T - QW:
                            kslots.free(keys_of[g][0], gathered[3])
                        first = nxt

            def values(srcT, weight, bias_row, blocks, ready):
                pe.wait(ready)
                for n, (k0, ksz) in enumerate(blocks):
                    i, free = pairs.take()
                    pe.wait(*free)
                    for k in range(KD):
                        nc.tensor.matmul(pair(i)[0:ksz, 0:D], srcT[:, k, k0:k0 + ksz], weight[:, k, :],
                                         start=(k == 0), stop=False)
                    m = pe.done(nc.tensor.matmul(pair(i)[0:ksz, 0:D], ones_row[:, 0:ksz], bias_row,
                                                 start=False, stop=True))
                    act.wait(m, va_ready)
                    m = act.done(nc.scalar.copy(
                        va[0:ksz, n, :, 0:HD], pair(i)[0:ksz, 0:D].rearrange("p (h d) -> p h d", d=HD)))
                    pairs.free(i, m)
                    pe.wait(m) if n == len(blocks) - 1 else None
                    yield 1

            cx = flat(raw[:])[0:SB, 0:2 * D].rearrange("p (n d) -> p n d", n=2)
            cT = flat(A[:])[:, 0:KD * S].rearrange("p (k s) -> p k s", k=KD)

            def cross_block(b):
                xb = X[:, b % 2]
                settle()
                w, w_m = load_weights(cross_table, w_room[:])
                ctx_in = load("ctx", cx, ctxt[b].rearrange("(n p) d -> p n d", p=SB))
                m = mean_var(st, mv, lambda t: xb[:, t, :], x_ready[b])
                m, r1 = yield from norm_scales(sc, mv, 1e-5, None, m)
                yield 3
                dve.wait(m)
                for t in range(TT):
                    m = normed(xs[:, t, :], xb[:, t, :], mv, t, r1)
                x_m = transpose_tokens(xT, xs, None, None, m)
                yield 4
                i, free = pairs.take()
                pe.wait(ctx_in, *free)
                for k in range(KD):
                    for n in range(2):
                        m = nc.tensor.transpose(pair(i)[:, k * BANK + n * SB:k * BANK + (n + 1) * SB],
                                                cx[:, n, k * P:(k + 1) * P], ident[0:SB, 0:SB])
                m = pe.done(m)
                act.wait(m)
                c_m = act.done(nc.scalar.copy(cT, pair(i).rearrange("p (k s) -> p k s", k=2)[:, :, 0:S]))
                pairs.free(i, c_m)
                blocks = [(0, SB), (SB, SB)]
                for ln in (pe, act, dve):
                    ln.wait(w_m)
                stored = []
                for m in split_projection("xk", stores["xk"][b], cT, w["xWk"], w["xbk"], S, c_m):
                    stored.append(m)
                    yield 1
                for m in split_projection("xq", stores["xq"][b], xT, w["xWq"], w["xbq"], T, x_m):
                    stored.append(m)
                    yield 3
                yield from values(cT, w["xWv"], w["xbv"], blocks, c_m)
                yield from attention(stores["xq"][b], stores["xk"][b], S, blocks, False, stored, w["xWo"], w["xbo"], xb, [x_ready[b]] * (TT * D // BANK))

            lg, top, ex, keep = (ab(n, [P, TT, e]) for n, e in (("lg", E), ("top", 8), ("ex", E), ("keep", E)))
            sm = ab("sm", [P, 2, TT])

            def self_block(b):
                xb = X[:, b % 2]
                settle()
                w, w_m = load_weights(self_table, w_room[:])
                m = mean_var(st, mv, lambda t: xb[:, t, :])
                m, r12 = yield from norm_scales(sc, mv, 1e-5, 1e-5, m)
                yield 3
                dve.wait(m)
                for t in range(TT):
                    normed(A[:, t, :], xb[:, t, :], mv, t, sc[:, 0, :])
                    m = normed(xs[:, t, :], xb[:, t, :], mv, t, r12)
                for ln in (pe, act, dve):
                    ln.wait(w_m)
                x_m = transpose_tokens(xT, xs, w["g1"], w["b1"], m)
                yield 5
                stored = []
                for m in split_projection("k", stores["k"][b], xT, w["Wk"], w["bk"], T, x_m):
                    stored.append(m)
                    yield 3
                for m in split_projection("q", stores["q"][b], xT, w["Wq"], w["bq"], T, x_m):
                    stored.append(m)
                    yield 3
                blocks = [(n * P, P) for n in range(TT)]
                yield from values(xT, w["Wv"], w["bv"], blocks, x_m)
                a_ready = [None] * (TT * D // BANK)
                yield from attention(stores["q"][b], stores["k"][b], T, blocks, True, stored, w["Wo"], w["bo"], A, a_ready)
                m = mean_var(st, mv, lambda t: A[:, t, :], *a_ready, *stored)
                m, r = yield from norm_scales(sc, mv, 1e-5, None, m)
                yield 3
                dve.wait(m)
                for t in range(TT):
                    m = normed(xs[:, t, :], A[:, t, :], mv, t, r)
                base_m = dve.done(nc.vector.tensor_tensor(flat(xb), flat(xb), flat(A[:]), ALU.add))
                h_m = transpose_tokens(xT, xs, w["g2"], w["b2"], m)
                far.close()
                h2 = h2s[b] = sb(f"h2_{b}", [P, KD, 2, T], F32R, at=far, side="right")
                act.wait(h_m)
                for k in range(KD):
                    m = act.done(nc.scalar.copy(h2[:, k, 0, :], xT[:, k, :]))
                    dve.wait(m)
                    h2_m = dve.done(nc.vector.tensor_tensor(
                        h2[:, k, 1, :], xT[:, k, :], h2[:, k, 0, :].bitcast(F32), ALU.subtract))
                yield 5
                i, free = pairs.take()
                pe.wait(h_m, *free)
                for t in range(TT):
                    o = pair(i)[:, t * E:(t + 1) * E]
                    for k in range(KD):
                        nc.tensor.matmul(o, xT[:, k, t * P:(t + 1) * P], w["Wr"][:, k, :],
                                         start=(k == 0), stop=False)
                    m = nc.tensor.matmul(o, ones_row[:], w["br"], start=False, stop=True)
                m = pe.done(m)
                dve.wait(m)
                m = dve.done(nc.vector.tensor_copy(flat(lg[:]), pair(i)[:, 0:TT * E]))
                pairs.free(i, m)
                dve.wait(m)
                for t in range(TT):
                    m = dve.done(nc.vector.max(top[:, t, :], lg[:, t, :]))
                dve.wait(m)
                dve.done(nc.vector.tensor_tensor(keep[:], lg[:], top[:, :, 1:2].to_broadcast([P, TT, E]),
                                                 ALU.is_ge))
                m = dve.done(nc.vector.tensor_tensor(lg[:], lg[:], top[:, :, 0:1].to_broadcast([P, TT, E]),
                                                     ALU.subtract))
                act.wait(m)
                m = act.done(nc.scalar.activation(ex[:], lg[:], ACT.Exp))
                dve.wait(m)
                m = dve.done(nc.vector.tensor_tensor(ex[:], ex[:], keep[:], ALU.mult))
                dve.wait(m)
                m = dve.done(nc.vector.tensor_reduce(sm[:, 0, :], ex[:], AX.X, ALU.add))
                dve.wait(m)
                m = dve.done(nc.vector.reciprocal(sm[:, 1, :], sm[:, 0, :]))
                dve.wait(m)
                m = dve.done(nc.vector.tensor_tensor(
                    WT[:, b], ex[:], sm[:, 1, :].unsqueeze(2).to_broadcast([P, TT, E]), ALU.mult))
                yield 4
                i, free = pairs.take()
                pe.wait(m, *free)
                for t in range(TT):
                    m = nc.tensor.transpose(pair(i)[0:E, t * P:(t + 1) * P], WT[:, b, t, :], ident[:])
                m = pe.done(m)
                wT = flat(xs[0:E, 0:T // D, :])
                dve.wait(m)
                m = dve.done(nc.vector.tensor_copy(wT, pair(i)[0:E]))
                pairs.free(i, m)
                pe.wait(m)
                for t0 in range(0, TT, 4):
                    i, free = pairs.take()
                    pe.wait(*free)
                    for t in range(t0, t0 + 4):
                        m = nc.tensor.matmul(pair(i)[:, (t - t0) * D:(t - t0 + 1) * D],
                                             wT[:, t * P:(t + 1) * P], w["eb2"], start=True, stop=True)
                    m = pe.done(m)
                    dve.wait(m, base_m)
                    dst4 = flat(xb[:, t0:t0 + 4, :])
                    m = dve.done(nc.vector.tensor_tensor(dst4, dst4, pair(i), ALU.add))
                    pairs.free(i, m)
                x_ready[b], h2_ready[b] = m, h2_m
                yield 3


            if stages >= 2:
                yield from cross_block(b)
            if stages >= 3:
                yield from self_block(b)

        def mixture(b, at):
            def mb(name, shape, dt=F32):
                return sb(f"{name}_{b}", shape, dt, at=at)

            w1 = mb("w1", [P, 2, KD, 2, FF], F32R)
            w2 = mb("w2", [P, 2, KF, 2, D], F32R)
            piece = mb("piece", [P, 2, BANK])
            LAG = 3
            mid = mb("mid", [P, LAG + 1, 2, BANK], F32R)
            gl = mb("gl", [P, 2, BANK])
            pieces, gls, hbanks, mids = Ring(2), Ring(2), Ring(2), Ring(LAG + 1)
            xb, h2 = X[:, b % 2], h2s[b]
            settle()
            w_free = {("w1", 0): None, ("w1", 1): None, ("w2", 0): None, ("w2", 1): None}
            w_ready = {}

            def expert_weights(e):
                W1, W2 = (io[n][e].rearrange("(k p) n -> p k n", p=P) for n in ("L0_ffn_e_w1", "L0_ffn_e_w2"))
                cuts = ([("w1", w1, W1, slice(k, k + 1), slice(n, n + BANK))
                         for k in range(KD) for n in range(0, FF, BANK)]
                        + [("w2", w2, W2, slice(k, k + BANK // D), slice(0, D))
                           for k in range(0, KF, BANK // D)])

                def bring(cut):
                    name, _, src, ks_, ns_ = cut
                    r, free = pieces.take()
                    to = piece[:, r, :].rearrange("p (k n) -> p k n", k=ks_.stop - ks_.start)
                    return r, to, load(f"piece{r}", to, src[:, ks_, ns_], *free)

                ahead = bring(cuts[0])
                for n, cut in enumerate(cuts):
                    name, dst, _, ks_, ns_ = cut
                    r, src, m = ahead
                    if n + 1 < len(cuts):
                        ahead = bring(cuts[n + 1])
                    hi, lo = dst[:, e % 2, ks_, 0, ns_], dst[:, e % 2, ks_, 1, ns_]
                    act.wait(m, w_free[name, e % 2])
                    m = act.done(nc.scalar.copy(hi, src))
                    pool.wait(m)
                    m = pool.done(nc.gpsimd.tensor_tensor(lo, src, hi.bitcast(F32), ALU.subtract))
                    pieces.free(r, m)
                    w_ready[name, e] = m
                    yield

            for _ in expert_weights(0):
                yield 3
            PARTS = ((0, 0), (0, 1), (1, 0))

            def up(e, c, f):
                i, free = hbanks.take()
                pe.wait(w_ready["w1", e], h2_ready[b], *free)
                h = PS[:, 6 + i, :]
                for k in range(KD):
                    for a, bb in PARTS:
                        m = nc.tensor.matmul(h, w1[:, e % 2, k, a, f * P:(f + 1) * P],
                                             h2[:, k, bb, c * BANK:(c + 1) * BANK],
                                             start=(k == 0 and (a, bb) == (0, 0)),
                                             stop=(k == KD - 1 and (a, bb) == PARTS[-1]))
                h_m = pe.done(m)
                g, free = gls.take()
                act.wait(h_m, *free)
                m = act.done(nc.scalar.activation(gl[:, g, :], h, ACT.Gelu, bias=eb1[:, e, f:f + 1]))
                hbanks.free(i, m)
                return h_m, g, m

            def down(e, f, acc, s, mid_m):
                pe.wait(mid_m, w_ready["w2", e])
                for t in range(BANK // P):
                    for a, bb in PARTS:
                        first = f == 0 and t % 2 == 0 and (a, bb) == (0, 0)
                        m = nc.tensor.matmul(acc[:, t * D:(t + 1) * D], mid[:, s, a, t * P:(t + 1) * P],
                                             w2[:, e % 2, f, bb, :],
                                             start=first, stop=(f == KF - 1 and (a, bb) == PARTS[-1]),
                                             skip_group_check=True)
                return pe.done(m)

            CH = T // BANK
            steps = [(e, c, f) for e in range(E) for c in range(CH) for f in range(KF)]
            made, x_m = {}, x_ready[b]
            weights = iter(())
            for n in range(len(steps) + LAG):
                if n < len(steps):
                    e, c, f = steps[n]
                    h_m, g, g_m = up(e, c, f)
                    if (c, f) == (CH - 1, KF - 1):
                        w_free["w1", e % 2] = h_m
                    if (c, f) == (CH - 1, 0) and e + 1 < E:
                        weights = expert_weights(e + 1)
                if n >= LAG:
                    e_, c_, f_ = steps[n - LAG]
                    if f_ == 0:
                        i, free = pairs.take()
                        pe.wait(*free)
                    s, m = made.pop(n - LAG)
                    d_m = down(e_, f_, pair(i), s, m)
                    mids.free(s, d_m)
                    if (c_, f_) == (CH - 1, KF - 1):
                        w_free["w2", e_ % 2] = d_m
                if n < len(steps):
                    s, free = mids.take()
                    dve.wait(g_m, *free)
                    m = dve.done(nc.vector.tensor_copy(mid[:, s, 0, :], gl[:, g, :]))
                    dve.wait(m)
                    m = dve.done(nc.vector.tensor_tensor(
                        mid[:, s, 1, :], gl[:, g, :], mid[:, s, 0, :].bitcast(F32), ALU.subtract))
                    gls.free(g, m)
                    made[n] = s, m
                    if f % 2 == 0:
                        next(weights, None)
                yield 2.6
                if n >= LAG and f_ == KF - 1:
                    dve.wait(d_m, x_m)
                    for t in range(BANK // P):
                        tile = c_ * BANK // P + t
                        m = dve.done(nc.vector.scalar_tensor_tensor(
                            xb[:, tile, :], pair(i)[:, t * D:(t + 1) * D],
                            WT[:, b, tile, e_:e_ + 1], xb[:, tile, :], ALU.mult, ALU.add))
                    pairs.free(i, m)
                    x_m = m
                    if e_ == E - 1:
                        tokens = slice(c_ * BANK, (c_ + 1) * BANK)
                        x_slot_free[b % 2] = load(
                            "out", out[b, tokens].rearrange("(t p) d -> p t d", p=P),
                            xb[:, c_ * BANK // P:(c_ + 1) * BANK // P, :], m)

        def load_weights(table, room=None, *marks):
            w, at = {}, 0
            for name, (shape, parts, zero) in table.items():
                if room is None:
                    t = sb(f"w_{name}", shape)[:]
                else:
                    size = 1
                    for n in shape[1:]:
                        size *= n
                    t = room[0:shape[0], at:at + size]
                    at += size
                    if len(shape) == 3:
                        t = t.rearrange("p (k n) -> p k n", k=shape[1])
                w[name] = t
                z_m = None
                if zero:
                    pool.wait(*marks)
                    z_m = pool.done(nc.gpsimd.memset(t, 0.0))
                for dst, src in parts(t):
                    w_m = load("weights", dst, src, z_m, *marks)
            return w, w_m

        def room_for(table):
            total = 0
            for shape, _, _ in table.values():
                size = 1
                for n in shape[1:]:
                    size *= n
                total += size
            return total

        def rows(name, k):
            src = io[name]
            return ([P, k, src.shape[1]], lambda t: [(t, src.rearrange("(k p) n -> p k n", p=P))], False)

        def column(name, k):
            return ([P, k], lambda t: [(t, io["cols_" + name])], False)

        def row(name):
            return ([1, io[name].shape[0]], lambda t: [(t, io[name].unsqueeze(0))], False)

        def head_rows(name):
            src = io[name]
            return ([P, G, D], lambda t: [(t[32 * j:32 * j + HD, :, :],
                                           src.rearrange("(g j d) n -> j d g n", j=HG, d=HD)[j])
                                          for j in range(HG)], True)

        mamba_table = {
            "norm": column("L0_attn_norm_w", KD), "in": rows("L0_attn_in_proj_w", KD),
            "bc": ([P, KI, 2 * N], lambda t: [
                (t[:, :, 0:N], io["L0_attn_B_proj_w"].rearrange("(k p) n -> p k n", p=P)),
                (t[:, :, N:2 * N], io["L0_attn_C_proj_w"].rearrange("(k p) n -> p k n", p=P))], False),
            "A": rows("L0_attn_A_proj_w", KI), "Ab_half": column("L0_attn_A_proj_b", KI),
            "Dw": column("L0_attn_D", KI), "out": rows("L0_attn_out_proj_w", KI),
            "abase_half": ([P, N], lambda t: [(t, io["L0_attn_A_base"].partition_broadcast(P))], False),
        }
        cross_table = {
            "xWq": rows("L0_xattn_Wq", KD), "xbq": column("L0_xattn_bq", KD),
            "xWk": rows("L0_xattn_Wk", KD), "xbk": column("L0_xattn_bk", KD),
            "xWv": rows("L0_xattn_Wv", KD), "xbv": row("L0_xattn_bv"),
            "xWo": head_rows("L0_xattn_Wo"), "xbo": row("L0_xattn_bo"),
        }
        self_table = {
            "g1": column("L0_ffn_ln1_g", KD), "b1": column("L0_ffn_ln1_b", KD),
            "g2": column("L0_ffn_ln2_g", KD), "b2": column("L0_ffn_ln2_b", KD),
            "Wq": rows("L0_ffn_Wq", KD), "bq": column("L0_ffn_bq", KD),
            "Wk": rows("L0_ffn_Wk", KD), "bk": column("L0_ffn_bk", KD),
            "Wv": rows("L0_ffn_Wv", KD), "bv": row("L0_ffn_bv"),
            "Wo": head_rows("L0_ffn_Wo"), "bo": row("L0_ffn_bo"),
            "Wr": rows("L0_ffn_Wr", KD), "br": row("L0_ffn_br"),
            "eb2": ([E, D], lambda t: [(t, io["L0_ffn_e_b2"])], False),
        }
        w_scan, w_m = load_weights(mamba_table)
        act.wait(load("eb1", eb1[:], io["cols_L0_ffn_e_b1"]))
        pe.wait(w_m)
        act.wait(w_m)
        m = act.done(nc.scalar.activation(w_scan["abase_half"], w_scan["abase_half"], ACT.Tanh, scale=0.5))
        dve.wait(m, w_m)
        m = dve.done(nc.vector.tensor_scalar(w_scan["abase_half"], w_scan["abase_half"], 0.25, 0.25,
                                             ALU.mult, ALU.add))
        m = dve.done(nc.vector.tensor_scalar(w_scan["Ab_half"], w_scan["Ab_half"], 0.5, None, ALU.mult))
        act.wait(m)
        scans, attns = Stream(), Stream()

        def after_scan(b):
            far = ExitStack()
            with ExitStack() as at:
                for step in attention_phase(b, at, far):
                    yield step * SHARE * SCAN_LENGTH / ATTENTION_LENGTH
            if stages >= 4:
                with ExitStack() as at:
                    for step in mixture(b, at):
                        yield step * (1 - SHARE) * SCAN_LENGTH / MIXTURE_LENGTH
                far.close()
            else:
                x_slot_free[b % 2] = load("out", out[b].rearrange("(t p) d -> p t d", p=P), X[:, b % 2],
                                          *attns.last.values(), x_ready[b])

        SCAN_LENGTH, ATTENTION_LENGTH, MIXTURE_LENGTH, SHARE = 415.0, 628.0, 365.0, 0.15
        for b in range(B + 1):
            tracks = []
            if b > 0:
                tracks.append((attns, after_scan(b - 1), 1.0))
            if b < B:
                tracks.append((scans, scan_block(b, w_scan), 1.0))
            for _ in weave(*tracks):
                pass
        sync.wait(*x_slot_free)


_COLUMNS = ["L0_attn_norm_w", "L0_attn_A_proj_b", "L0_attn_D", "L0_xattn_bq", "L0_xattn_bk",
            "L0_ffn_ln1_g", "L0_ffn_ln1_b", "L0_ffn_ln2_g", "L0_ffn_ln2_b", "L0_ffn_bq", "L0_ffn_bk"]
_OUT_SHAPE = (4, 1024, 256)


def kernel(**inputs):
    import numpy as np
    import concourse.bacc as bacc
    from concourse.bass_utils import run_bass_kernel_spmd as run

    nc = bacc.Bacc("TRN2", target_bir_lowering=False, num_devices=1)
    r = np.arange(128)
    consts = {
        "c_ident": np.eye(128, dtype=np.float32),
        "c_masks": np.stack([np.where(r[None, :] > r[:, None], MASKED, 0.0),
                             np.where(r[:, None] > r[None, :], MASKED, 0.0)], 1).astype(np.float32),
        "c_sel": (r[:, None] == 32 * np.arange(4)[None, :] + 16).astype(np.float32),
        "c_zeros": np.zeros((3, 1024), np.float32),
        "c_ones": np.ones((1, 128), np.float32),
    }
    columns = {"cols_" + name: np.asarray(inputs[name]).reshape(-1, 128).T for name in _COLUMNS}
    eb1 = np.asarray(inputs["L0_ffn_e_b1"])
    columns["cols_L0_ffn_e_b1"] = eb1.reshape(eb1.shape[0], -1, 128).transpose(2, 0, 1)
    arrays, io = {}, {}
    for name, value in {**inputs, **columns, **consts}.items():
        a = np.ascontiguousarray(value)
        arrays["in_" + name] = a
        io[name] = nc.dram_tensor("in_" + name, a.shape, mybir.dt.from_np(a.dtype), kind="ExternalInput").ap()
    out = nc.dram_tensor("out_x", _OUT_SHAPE, F32, kind="ExternalOutput").ap()
    decoder_layer(nc, io, out, STAGES)
    result = run(nc, [arrays], core_ids=[0])
    return result.results[0]["out_x"]
```
